# Optimizing a Trainium2 kernel written in Bass

```python
import numpy as np
import jax
import jax.numpy as jnp

def _softmax(x, axis=-1):
    return jax.nn.softmax(x, axis=axis)

def _gelu(x):
    return jax.nn.gelu(x, approximate=True)

def _silu(x):
    return jax.nn.silu(x)

def _sigmoid(x):
    return jax.nn.sigmoid(x)

def _layernorm(x, axis=-1, eps=1e-05):
    m = jnp.mean(x, axis=axis, keepdims=True)
    v = jnp.var(x, axis=axis, keepdims=True)
    return (x - m) / jnp.sqrt(v + eps)

def _scatter_add(tgt, idx, src, axis=0):
    return tgt.at[idx].add(src)

def _segment_sum(src, seg, n):
    return jax.ops.segment_sum(src, seg, n)
kernel_name = 'mk_prb_d1_jaxref_r4_d2ff12'

def setup_inputs(seed: int=0):
    np.random.seed(seed)
    _w = jnp.asarray

    def _L0_attn_setup():
        import jax, jax.numpy as jnp
        import numpy as np
        B, S, E, H = (2, 512, 256, 16)
        D = E // H
        NEG_INF = -1e+30

        def alibi_slopes(n_head):
            return jnp.asarray([2.0 ** (-8.0 * (i + 1) / n_head) for i in range(n_head)], dtype=jnp.float32)
        key = jax.random.key(seed)
        ks = jax.random.split(key, 5)
        scale = 0.02
        return {'x': jax.random.normal(ks[0], (B, S, E), dtype=jnp.float32), 'W_kqv': jax.random.normal(ks[1], (E, 3 * E), dtype=jnp.float32) * scale, 'b_kqv': jnp.zeros((3 * E,), dtype=jnp.float32), 'W_proj': jax.random.normal(ks[2], (E, E), dtype=jnp.float32) * scale, 'b_proj': jnp.zeros((E,), dtype=jnp.float32), 'slopes': alibi_slopes(H)}
    _L0_attn_in = _L0_attn_setup()

    def _L0_ffn_setup():
        import jax, jax.numpy as jnp
        import numpy as np
        key = jax.random.key(seed)
        k0, k1, k2, k3 = jax.random.split(key, 4)
        B, S, D, F, E = (8, 512, 256, 512, 8)
        x = jax.random.normal(k0, (B, S, D), dtype=jnp.float32)
        Wg = jax.random.normal(k1, (D, E), dtype=jnp.float32) * 0.02
        W1 = jax.random.normal(k2, (E, D, F), dtype=jnp.float32) * 0.02
        W2 = jax.random.normal(k3, (E, F, D), dtype=jnp.float32) * 0.02
        return {'x': x, 'Wg': Wg, 'W1': W1, 'W2': W2}
    _L0_ffn_in = _L0_ffn_setup()
    _d = {'L0_attn_x': _L0_attn_in['x'], 'L0_attn_W_kqv': _L0_attn_in['W_kqv'], 'L0_attn_b_kqv': _L0_attn_in['b_kqv'], 'L0_attn_W_proj': _L0_attn_in['W_proj'], 'L0_attn_b_proj': _L0_attn_in['b_proj'], 'L0_attn_slopes': _L0_attn_in['slopes'], 'L0_ffn_Wg': _L0_ffn_in['Wg'], 'L0_ffn_W1': _L0_ffn_in['W1'], 'L0_ffn_W2': _L0_ffn_in['W2']}
    _x0 = _d['L0_attn_x']
    _d['L0_attn_x'] = jax.random.normal(jax.random.fold_in(jax.random.key(seed), 1), (8, 512, 256), dtype=_x0.dtype)
    del _x0
    return _d

def reference(L0_attn_x, L0_attn_W_kqv, L0_attn_b_kqv, L0_attn_W_proj, L0_attn_b_proj, L0_attn_slopes, L0_ffn_Wg, L0_ffn_W1, L0_ffn_W2):

    def _L0_attn_ref(x, W_kqv, b_kqv, W_proj, b_proj, slopes):
        import jax, jax.numpy as jnp
        import numpy as np
        B, S, E, H = (2, 512, 256, 16)
        D = E // H
        NEG_INF = -1e+30

        def alibi_slopes(n_head):
            return jnp.asarray([2.0 ** (-8.0 * (i + 1) / n_head) for i in range(n_head)], dtype=jnp.float32)
        b, s, e = x.shape
        kqv = x @ W_kqv + b_kqv
        k, q, v = jnp.split(kqv, 3, axis=-1)
        k = k.reshape(b, s, H, D)
        q = q.reshape(b, s, H, D)
        v = v.reshape(b, s, H, D)
        attn = jnp.einsum('bqhd,bkhd->bhqk', q, k) * (1.0 / jnp.sqrt(jnp.float32(D)))
        i = jnp.arange(s)[:, None]
        j = jnp.arange(s)[None, :]
        rel = (j - i).astype(jnp.float32)
        bias = slopes[:, None, None] * jnp.tril(rel)
        bias = jnp.where(j > i, NEG_INF, bias)
        attn = jax.nn.softmax(attn + bias[None], axis=-1)
        y = jnp.einsum('bhqk,bkhd->bqhd', attn, v).reshape(b, s, e)
        return y @ W_proj + b_proj

    def _L0_ffn_ref(x, Wg, W1, W2):
        import jax, jax.numpy as jnp
        import numpy as np
        B, S, D = x.shape
        E = Wg.shape[1]
        T = B * S
        cap = max(1, T // E)
        xt = x.reshape(T, D)
        logits = xt @ Wg
        probs = jax.nn.softmax(logits, axis=-1)
        pT = probs.T
        _, top_idx = jax.lax.top_k(pT, cap)
        sel = jnp.zeros((E, T), dtype=bool).at[jnp.arange(E)[:, None], top_idx].set(True)
        masked = jnp.where(sel, pT, -jnp.inf)
        assigned = sel.any(axis=0)
        tok2exp = jnp.where(assigned, jnp.argmax(masked, axis=0), jnp.argmax(pT, axis=0))
        weights = jnp.take_along_axis(probs, tok2exp[:, None], axis=1)[:, 0]
        out = jnp.zeros_like(xt)
        for e in range(E):
            gate = jnp.where(tok2exp == e, weights, 0.0)
            h = jax.nn.gelu(xt @ W1[e], approximate=False) @ W2[e]
            out = out + gate[:, None] * h
        return out.reshape(B, S, D)
    x = L0_attn_x
    xn = _layernorm(x, axis=-1)
    x = x + _L0_attn_ref(xn, L0_attn_W_kqv, L0_attn_b_kqv, L0_attn_W_proj, L0_attn_b_proj, L0_attn_slopes) + _L0_ffn_ref(xn, L0_ffn_Wg, L0_ffn_W1, L0_ffn_W2)
    return x

_drawn_inputs = setup_inputs


def setup_inputs(seed=0):
    import zlib

    import numpy as np

    out = dict(_drawn_inputs(seed))
    spreads = {'L0_attn_b_kqv': (0.0, 0.278), 'L0_attn_b_proj': (0.0, 0.1)}
    factors = {'L0_ffn_Wg': 4.0, 'L0_ffn_W1': 3.803, 'L0_ffn_W2': 3.721, 'L0_attn_slopes': 2.909}
    for name, (base, spread) in spreads.items():
        noise = np.random.default_rng([zlib.crc32(name.encode()), seed]).standard_normal(out[name].shape)
        drawn = base * np.exp(spread * noise) if base else spread * noise
        out[name] = jnp.asarray(drawn.astype(out[name].dtype))
    for name, factor in factors.items():
        out[name] = (out[name] * factor).astype(out[name].dtype)
    return out
```

```python
from contextlib import ExitStack

import concourse.bass as bass
from concourse import mybir

F32, F16, BF16 = mybir.dt.float32, mybir.dt.float16, mybir.dt.bfloat16
I32, U32 = mybir.dt.int32, mybir.dt.uint32
ALU = mybir.AluOpType
ACT = mybir.ActivationFunctionType
AX = mybir.AxisListType.X

P = 128
B, S, E, H, D = 8, 512, 256, 16, 16
T = B * S
NT = T // P
TB = S // P
EC = E // P
X, FF = 8, 512
FC = FF // P
CAP = T // X
TILES = NT + X
HG = 4
NG = H // HG
WS = 256.0
SCORE = 1.0 / (4.0 * WS * WS)
NEG = -1e30 / SCORE
EPS = 1e-5
PARTS = 3
Q_ROWS = (0, 0, 0, 1, 1, 2)
K_ROWS = (0, 1, 2, 0, 1, 0)
R_ALIBI = len(Q_ROWS) * D
R_SHIFT = R_ALIBI + 3
R_FAR = R_SHIFT + 2
FAR = -(-S // (P - R_FAR + 1))
MID = 256
VW = D + 1
ROW = 2 * E + 4
BITS = 30
BIS = (2, 1, 2, 1)
BPB = sum(BIS)
LOOPED = 6
NO_TOKEN = 1 << 20
UNITS = [(3, (h,)) for h in range(4)] + [(2, (h,)) for h in range(4)] + \
        [(1, (0, 1)), (1, (2, 3)), (0, (0, 1, 2, 3))]
NU = len(UNITS)
NSJ = 3 * HG
W_DIAG, W_R0, W_R1, W_R2 = 0, 512, 896, 1152
W_ALL = 1280
PIECES = [(0, W_R0, 128, 384), (0, 0, 0, 128), (1, W_R1, 256, 256), (2, W_R2, 384, 128),
          (1, 128, 128, 128), (2, 256, 256, 128), (3, 384, 384, 128)]


def layer(nc, x, w_kqv, b_kqv, w_proj, b_proj, slopes, wg, w1, w2, out):
    x_t = x.rearrange("b (t p) e -> b p t e", p=P)
    qk_d = [nc.dram_tensor(f"{n}_parts", [PARTS, H * D, T], BF16, kind="Internal").ap() for n in "kq"]
    v_d = nc.dram_tensor("v_rows", [B, P, TB * H * VW], F32, kind="Internal").ap()
    xa_d = nc.dram_tensor("x_plus_attention", [T, E], F32, kind="Internal").ap()
    ws_d = nc.dram_tensor("expert_parts", [X, P, 2, 2, 1024], F16, kind="Internal").ap()
    xs_d = nc.dram_tensor("sorted_rows", [TILES * P, ROW // 2], I32, kind="Internal").ap()
    out_rows = out.rearrange("b s e -> (b s) e")
    xa_t = xa_d.rearrange("(b t p) e -> b p t e", p=P, t=TB)

    with ExitStack() as ctx:
        def sb(name, shape, dt):
            return ctx.enter_context(nc.sbuf_tensor(name, shape, dt))

        def sem(name):
            return ctx.enter_context(nc.semaphore(name))

        def sems(name, n=2):
            return [sem(f"{name}{i}") for i in range(n)]

        ps = ctx.enter_context(nc.psum_tensor("ps", [P, 8, 512], F32))
        bank = [ps[:, i, :] for i in range(8)]

        id16 = sb("id16", [P, P], F16)
        idb = sb("idb", [P, P], BF16)
        idf = sb("idf", [P, P], F32)
        ones = sb("ones", [P, P], BF16)
        tri = sb("tri", [P, P], BF16)
        maxmask = sb("maxmask", [P, P], BF16)
        spread = sb("spread", [P, P], F32)
        bits = sb("bits", [P, LOOPED * BPB, X], U32)
        epst = sb("epst", [P, 1], F32)
        seg = sb("seg", [P, X, NT], F32)
        rank8 = sb("rank8", [P, X, NT], F32)
        lim = sb("lim", [P, X, NT], F32)
        sno = sb("sno", [P, TILES, X], F32)
        iot = sb("iot", [P, TILES * X], I32)
        tok = sb("tok", [P, NT], I32)
        w_h = sb("w_h", [P, EC, 3 * E + X], F16)
        w_l = sb("w_l", [P, EC, 3 * E + X], F16)
        bqk = sb("bqk", [P, 4], F32)
        bv = sb("bv", [P, H, D], F32)
        bp = sb("bp", [P, E], F32)
        wp = sb("wp", [P, NG, E], F32)
        sl = sb("sl", [P, 7, H], F32)
        slb = sb("slb", [P, 3, H], BF16)
        qs = sb("qs", [P, 2, NG, HG, S], BF16)
        ks = sb("ks", [P, 2, NG, HG, S], BF16)
        pr_all = sb("pr_all", [P, 8, W_ALL], F32)
        vt = sb("vt", [P, 2, TB, H, VW], F32)
        xnp = sb("xnp", [P, NT, ROW], F16)
        ysb = sb("ysb", [P, 2, S], F32)
        rec = sb("rec", [P, 2, S], F32)
        yn = sb("yn", [P, NG, S], F32)
        xr = sb("xr", [P, 2, TB, E], F32)
        mx = sb("mx", [P, 2, TB, H], F32)
        cc = sb("cc", [H, 2, 2, S], BF16)
        lg = sb("lg", [P, NT, X], F32)
        pe8 = sb("pe8", [P, NT, X], F32)
        pr = sb("pr", [P, X, NT], F32)
        thr = sb("thr", [P, X], F32)
        cand = sb("cand", [P, X], F32)
        hit = sb("hit", [P, X, NT], BF16)
        cnt = sb("cnt", [P, X], BF16)
        acc = sb("acc", [P, X], U32)
        r32 = sb("r32", [P, 6, NT], F32)
        r8 = sb("r8", [P, 6, X], F32)
        rr = [sb(f"rr{i}", [P, X, NT], F32) for i in range(3)]
        gtb = sb("gtb", [P, X, NT], BF16)
        pos = sb("pos", [P, NT], I32)
        ecmp = sb("ecmp", [P, TILES, X], F32)
        eidf = sb("eidf", [P, TILES], F32)
        eid = sb("eid", [P, TILES], I32)

        flat = pr_all[:, :, :].rearrange("p a b -> p (a b)")
        at = [0]

        def cut(n_bytes, dt, pattern=None, **dims):
            n = n_bytes // 4
            v = flat[:, at[0]:at[0] + n]
            at[0] += n
            assert at[0] <= 8 * W_ALL
            v = v if dt == F32 else v.bitcast(dt)
            return v.rearrange(pattern, **dims) if pattern else v

        xin = [cut(4096, F32, "p (t e) -> p t e", t=TB) for _ in range(2)]
        xn = cut(4096, F32, "p (t e) -> p t e", t=TB)
        xw = [cut(4096, F16, "p (t e) -> p t e", t=TB) for _ in range(2)]
        xt = [cut(4096, F16, "p (a k n) -> p a k n", a=2, k=EC) for _ in range(2)]
        r1 = [cut(2048, F32) for _ in range(2)]
        bst = sb("bst", [P, TB, 6], F32)
        mv = sb("mv", [P, TB, 2], F32)
        std = sb("std", [P, TB], F32)
        rstd = sb("rstd", [P, TB], F32)
        pt = [ks[:, 1, c, 0:PARTS, :] for c in range(4)]
        wst = qs[:, 1, 0:2, :, :].rearrange("p a b c -> p (a b c)").bitcast(F32)
        wsp = [qs[:, 1, 2 + j, :, :].rearrange("p b c -> p (b c)").bitcast(F16) for j in range(2)]
        wk_f = qs[:, 0, 0:2, :, :].rearrange("p a b c -> p (a b c)").bitcast(F32)[:, 0:EC * (3 * E + X)] \
            .rearrange("p (k c) -> p k c", k=EC)

        w1_sb = xnp[:, :, :].rearrange("p a b -> p (a b)")[:, 0:X * 2 * 1024] \
            .rearrange("p (x a w) -> p x a w", x=X, a=2)
        w2_h = qs[:, 0, :, :, :].rearrange("p a b c -> p (a b c)").bitcast(F16) \
            .rearrange("p (x w) -> p x w", x=X)
        w2_l = ks[:, 0, :, :, :].rearrange("p a b c -> p (a b c)").bitcast(F16) \
            .rearrange("p (x w) -> p x w", x=X)
        at[0] = 0
        xs_sb = cut(2 * ROW * 2, F16, "p (q c) -> p q c", q=2)
        xT = cut(2 * 4 * P * 2, F16, "p (q a c) -> p q a c", q=2, a=4)
        hg = cut(2 * FF * 4, F32, "p (q c) -> p q c", q=2)
        hh = cut(2 * 2 * FF * 2, F16, "p (q a c) -> p q a c", q=2, a=2)
        xg = cut(2 * E * 4, F32, "p (q c) -> p q c", q=2)
        ob = cut(2 * E * 4, F32, "p (q c) -> p q c", q=2)
        empty = sb("empty", [P, ROW], F16)

        const_made = sem("const_made")
        pool_step = sem("pool_step")
        cst_in = sem("cst_in")
        dve_step = sem("dve_step")
        act_step = sem("act_step")
        w_split = sem("w_split")
        x_in, x_made = sems("x_in"), sem("x_made")
        stats = sem("stats")
        std_made = sem("std_made")
        xw_made = sem("xw_made")
        xnp_in = sems("xnp_in")
        t_made, t_used = sem("t_made"), sem("t_used")
        qk_made, hi_made, r1_made, mid_made, lo_made = (sem(n) for n in ("qk_made", "hi_made", "r1_made", "mid_made", "lo_made"))
        parts_out = sems("parts_out", 4)
        v_made, v_used = sem("v_made"), sem("v_used")
        v_out = sems("v_out")
        we_in, we_hi, we_lo, we_out = sem("we_in"), sem("we_hi"), sem("we_lo"), sem("we_out")
        q8 = sem("q8")
        rows_made, rows_in = sem("rows_made"), sem("rows_in")
        exp8 = sem("exp8")
        grp_in = [sems(f"grp_in{p}_", NG) for p in range(2)]
        vb_in = sems("vb_in")
        xr_in, xr_made, xa_out = sems("xr_in"), sem("xr_made"), sems("xa_out")
        sm_made, max_made = sem("sm_made"), sem("max_made")
        ct_made, c_made, c_in = sem("ct_made"), sem("c_made"), sems("c_in")
        s_made, exp_made, sel_made = sem("s_made"), sem("exp_made"), sem("sel_made")
        y_made, y_copied, sum_made, div_made = sem("y_made"), sem("y_copied"), sem("sum_made"), sem("div_made")
        pj_made, xadd_made = sem("pj_made"), sem("xadd_made")
        cnt_made, tot_made = sem("cnt_made"), sem("tot_made")
        rt_dve, rt_pe = sem("rt_dve"), sem("rt_pe")
        pos_made, scattered, list_init, w1_in, w2_in = sem("pos_made"), sem("scattered"), sem("list_init"), sem("w1_in"), sem("w2_in")
        xs_in, tt_made, xT_made, h_made, hg_made, hh_made, hl_made, o_made, ob_made = (
            sems("xs_in"), sem("tt_made"), sem("xT_made"), sem("h_made"), sem("hg_made"), sem("hh_made"),
            sem("hl_made"), sem("o_made"), sem("ob_made"))
        xg_in, ob_out = sems("xg_in"), sems("ob_out")
        empt = sem("empt")

        rec_made = sem("rec_made")
        shift_step = sem("shift_step")
        consts = sem("consts")
        apart = sem("apart")

        block = ctx.enter_context(nc.Block())

        def after(eng, signal, value):
            if not isinstance(value, int) or value > 0:
                eng.wait_ge(signal, value)

        def wait_apart(eng, signal, value):
            eng.wait_ge(signal, value)
            eng.sem_inc(apart, 1)

        def pairs(eng, count, body, first=0):
            with eng.Fori(first, first + count) as i:
                for p in range(2):
                    body(i * 2 + p, i, p)

        def stage_a(eng, body):
            for n in (0, 1):
                body(n, 0, n)
            pairs(eng, B // 2 - 1, body, 1)

        def last_two(body):
            for n in (B - 2, B - 1):
                body(n, n // 2, n % 2)

        @block.sync
        def _(sp):
            sp.dma_start(wk_f[:, :, 0:3 * E], w_kqv.rearrange("(k p) c -> p k c", p=P)).then_inc(cst_in, 16)
            sp.dma_start(wk_f[:, :, 3 * E:], wg.rearrange("(k p) c -> p k c", p=P)).then_inc(cst_in, 16)
            sp.dma_start(bqk[:, :], b_kqv[0:2 * E].rearrange("(c p) -> p c", p=P), allow_slow_non_contiguous=True).then_inc(cst_in, 16)
            sp.dma_start(bv[:, :, :].rearrange("p h d -> p (h d)"),
                         b_kqv[2 * E:3 * E].partition_broadcast(P)).then_inc(cst_in, 16)
            sp.dma_start(bp[:, :], b_proj.partition_broadcast(P)).then_inc(cst_in, 16)
            sp.dma_start(sl[R_ALIBI:R_ALIBI + 3, 0, :], slopes.partition_broadcast(3)).then_inc(cst_in, 16)
            sp.wait_ge(const_made, 12)
            for j in range(HG):
                sp.dma_start(wp[32 * j:32 * j + D, :, :],
                             w_proj.rearrange("(g j d) n -> j d g n", g=NG, d=D)[j]).then_inc(cst_in, 16)

            def store(n, p):
                sp.wait_ge(xw_made, n + 1)
                sp.dma_start(xnp[:, bass.ds(n * TB, TB), 0:2 * E], xw[p]).then_inc(xnp_in[p], 16)
                sp.wait_ge(we_lo, n + 1)
                for j in range(2):
                    sp.dma_start(ws_d[bass.ds(n, 1), :, j].rearrange("x p a w -> p (x a) w"),
                                 wsp[j].rearrange("p (a w) -> p a w", a=2)).then_inc(we_out, 16)
                for c in range(4):
                    sp.wait_ge(lo_made, 4 * n + c + 1)
                    for s in range(PARTS):
                        sp.dma_start(qk_d[c // 2][s, (c % 2) * P:(c % 2 + 1) * P, bass.ds(n * S, S)],
                                     pt[c][:, s, :]).then_inc(parts_out[c], 16)
                sp.wait_ge(v_used, 4 * n + 4)
                sp.dma_start(v_d[bass.ds(n, 1)].rearrange("b p c -> p (b c)"),
                             vt[:, p].rearrange("p t h w -> p (t h w)")).then_inc(v_out[p], 16)

            def a(n, i, p):
                after(sp, x_made, n - 1)
                sp.dma_start(xin[p], x_t[bass.ds(n, 1)].rearrange("b p t e -> p (b t) e")).then_inc(x_in[p], 16)
                after(sp, we_lo, n)
                sp.dma_start(wst[:, 0:1024].rearrange("p (k f) -> p k f", k=EC),
                             w1[bass.ds(n, 1)].rearrange("x (k p) f -> p (x k) f", p=P)).then_inc(we_in, 16)
                sp.dma_start(wst[:, 1024:2048].rearrange("p (k f) -> p k f", k=FC),
                             w2[bass.ds(n, 1)].rearrange("x (k p) f -> p (x k) f", p=P)).then_inc(we_in, 16)
                if not isinstance(n, int) or n > 0:
                    store(n - 1, 1 - p)

            stage_a(sp, a)
            store(B - 1, 1)

            def load_group(n, p, g):
                for r in range(len(Q_ROWS)):
                    for st, which, rows in ((qs, 1, Q_ROWS), (ks, 0, K_ROWS)):
                        sp.dma_start(st[r * D:(r + 1) * D, p, g, :, :],
                                     qk_d[which][rows[r], g * HG * D:(g + 1) * HG * D, bass.ds(n * S, S)]
                                     .rearrange("(h d) n -> d h n", d=D)).then_inc(grp_in[p][g], 16)

            def load_v(n, p):
                sp.dma_start(vt[:, p].rearrange("p t h w -> p (t h w)"),
                             v_d[bass.ds(n, 1)].rearrange("b p c -> p (b c)")).then_inc(vb_in[p], 16)

            def load_x(n, p):
                sp.dma_start(xr[:, p], x_t[bass.ds(n, 1)].rearrange("b p t e -> p (b t) e")).then_inc(xr_in[p], 16)

            for c in range(4):
                sp.wait_ge(parts_out[c], 16 * PARTS * B)
            for p in range(2):
                sp.wait_ge(v_out[p], 16 * B // 2)
            sp.wait_ge(we_out, 32 * B)
            sp.wait_ge(rows_made, 1)
            for st in (qs, ks):
                sp.dma_start(st[R_ALIBI:P, 1], st[R_ALIBI:P, 0]).then_inc(rows_in, 16)
            for p in range(2):
                for g in range(NG):
                    load_group(p, p, g)
                load_v(p, p)
                load_x(p, p)

            def b(n, i, p, more=True):
                for g in range(NG):
                    if more:
                        sp.wait_ge(s_made, NSJ * (NG * n + g + 1))
                        load_group(n + 2, p, g)
                if more:
                    sp.wait_ge(y_made, NG * n + NG + 2)
                    load_v(n + 2, p)
                sp.wait_ge(xadd_made, 2 * n + 2 + 1)
                sp.dma_start(xa_t[bass.ds(n, 1)].rearrange("b p t e -> p (b t) e"), xr[:, p]).then_inc(xa_out[p], 16)
                if more:
                    sp.wait_ge(xa_out[p], 16 * (i + 1))
                    load_x(n + 2, p)

            pairs(sp, LOOPED // 2, b)
            sp.wait_ge(scattered, 16 * NT)
            for a_ in range(2):
                sp.dma_start(w1_sb[:, :, a_, :], ws_d[:, :, a_, 0, :].rearrange("x p w -> p x w")).then_inc(w1_in, 16)
            b(B - 2, B // 2 - 1, 0, False)
            sp.wait_ge(s_made, NSJ * NG * (B - 1))
            sp.dma_start(w2_h, ws_d[:, :, 0, 1, :].rearrange("x p w -> p x w")).then_inc(w2_in, 16)
            sp.dma_start(w2_l, ws_d[:, :, 1, 1, :].rearrange("x p w -> p x w")).then_inc(w2_in, 16)
            b(B - 1, B // 2 - 1, 1, False)

            def load_tile(s, k, q):
                sp.dma_start(xs_sb[:, q, :].bitcast(I32), xs_d[bass.ds(s * P, P), :]).then_inc(xs_in[q], 16)

            load_tile(0, 0, 0)
            load_tile(1, 0, 1)
            with sp.Fori(0, (TILES - 2) // 2) as k:
                for q in range(2):
                    sp.wait_ge(ob_out[q], 16 * (k + 1))
                    load_tile(2 * k + 2 + q, k + 1, q)
            for q in range(2):
                sp.wait_ge(ob_out[q], 16 * (TILES // 2))

        @block.gpsimd
        def _(pool):
            step = [0]

            def mark(ins):
                step[0] += 1
                ins.then_inc(pool_step, 1)
                pool.wait_ge(pool_step, step[0])

            mark(pool.memset(epst[:, :], EPS))
            for m in (id16, idb, idf, spread):
                pool.memset(m[:, :], 0.0).then_inc(pool_step, 1)
            pool.memset(ones[:, :], 1.0).then_inc(pool_step, 1)
            pool.memset(tri[:, :], 1.0).then_inc(pool_step, 1)
            pool.memset(maxmask[:, :], 0.0).then_inc(pool_step, 1)
            step[0] += 7
            mark(pool.memset(wp[:, :, :], 0.0))
            pool.sem_inc(const_made, 1)
            for m in (id16, idb, idf):
                pool.affine_select(out=m[:, :], in_=m[:, :], compare_op=ALU.not_equal, fill=1.0, base=0,
                                   pattern=[[-1, P]], channel_multiplier=1).then_inc(const_made, 1)
            v = spread[:, :].rearrange("p (j r) -> p j r", j=4)
            pool.affine_select(out=v, in_=v, compare_op=ALU.not_equal, fill=1.0, base=-D,
                               pattern=[[-32, 4], [0, 32]], channel_multiplier=1).then_inc(const_made, 1)
            pool.affine_select(out=tri[:, :], in_=tri[:, :], compare_op=ALU.is_ge, fill=0.0, base=-1,
                               pattern=[[1, P]], channel_multiplier=-1).then_inc(const_made, 1)
            pool.affine_select(out=maxmask[:, :], in_=maxmask[:, :], compare_op=ALU.is_ge, fill=NEG, base=0,
                               pattern=[[-1, P]], channel_multiplier=1).then_inc(const_made, 1)
            pool.memset(seg[:, :, :], 1.0).then_inc(const_made, 1)
            for p in range(2):
                pool.memset(vt[:, p].rearrange("p t h w -> p (t h) w")[:, :, D:VW], 1.0).then_inc(const_made, 1)
            pool.memset(empty[:, :], 0.0).then_inc(const_made, 1)
            pool.memset(thr[:, :], 0.0).then_inc(const_made, 1)
            base = 12
            def ints(pattern, n, b0, out_ap, chan=0):
                mark(pool.iota(iot[:, 0:n], pattern=pattern, base=b0, channel_multiplier=chan))
                mark(pool.tensor_copy(out_ap, iot[:, 0:n]))

            ints([[-1, X], [0, NT]], X * NT, X, rank8[:, :, :].rearrange("p a b -> p (a b)"))
            ints([[0, X], [P, NT]], X * NT, 0, lim[:, :, :].rearrange("p a b -> p (a b)"))
            ints([[1, TILES], [0, X]], TILES * X, 0, sno[:, :, :].rearrange("p a b -> p (a b)"))
            mark(pool.iota(tok[:, :], pattern=[[P, NT]], base=0, channel_multiplier=1))
            pool.wait_ge(const_made, base)
            mark(pool.memset(seg[:, :, 0:1], 0.0))
            mark(pool.memset(bits[:, :, :], 0))
            for k in range(BITS):
                pool.memset(bits[:, k, :], 1 << (BITS - 1 - k)).then_inc(pool_step, 1)
            step[0] += BITS
            mark(pool.memset(empty[:, 2 * E:2 * E + 2].bitcast(I32), NO_TOKEN))
            pool.sem_inc(consts, 1)
            pool.dma_start(xs_d.rearrange("(s p) c -> p s c", p=P),
                           empty[:, :].bitcast(I32)[:, None, :].broadcast_to([P, TILES, ROW // 2])).then_inc(list_init, 16)

            rows = slice(R_ALIBI, P)
            kt, qt = ysb[rows, 0, :], ysb[rows, 1, :]
            b0 = (R_FAR - 1 - R_ALIBI) * FAR
            mark(pool.memset(ysb[rows, :, :], 1.0))
            mark(pool.affine_select(out=kt, in_=kt, compare_op=ALU.is_ge, fill=0.0, base=b0,
                                    pattern=[[1, S]], channel_multiplier=-FAR))
            mark(pool.affine_select(out=kt, in_=kt, compare_op=ALU.is_ge, fill=0.0, base=FAR - 1 - b0,
                                    pattern=[[-1, S]], channel_multiplier=FAR))
            mark(pool.memset(ysb[R_ALIBI:R_FAR, 0, :], 1.0))
            mark(pool.iota(rec[R_ALIBI:R_SHIFT, 0, :].bitcast(I32), pattern=[[1, S]], base=-MID, channel_multiplier=0))
            mark(pool.tensor_copy(ysb[R_ALIBI:R_SHIFT, 0, :], rec[R_ALIBI:R_SHIFT, 0, :].bitcast(I32)))
            mark(pool.memset(ysb[rows, 1, :], 0.0))
            mark(pool.affine_select(out=qt, in_=qt, compare_op=ALU.is_ge, fill=NEG, base=b0,
                                    pattern=[[1, S]], channel_multiplier=-FAR))
            pool.wait_ge(w_split, 2)
            pool.wait_ge(q8, 1)
            rows_base = step[0]

            def a(n, i, p):
                after(pool, lo_made, 4 * n)
                if p == 0:
                    pool.tensor_copy(ks[rows, 0, bass.ds(i, 1)].rearrange("p g h n -> p (g h) n"),
                                     kt[:, None, :].broadcast_to([P - R_ALIBI, HG, S])).then_inc(pool_step, 1)
                    pool.wait_ge(pool_step, i * 3 + (rows_base + 1))
                else:
                    pool.tensor_copy(qs[rows, 0, bass.ds(i, 1)].rearrange("p g h n -> p (g h) n"),
                                     qt[:, None, :].broadcast_to([P - R_ALIBI, HG, S])).then_inc(pool_step, 1)
                    pool.wait_ge(pool_step, i * 3 + (rows_base + 2))
                    pool.tensor_copy(qs[R_ALIBI:R_SHIFT, 0, bass.ds(i, 1)].rearrange("p g h n -> p (g h) n"),
                                     sl[R_ALIBI:R_SHIFT, 6, bass.ds(i * HG, HG)][:, :, None].broadcast_to([3, HG, S])
                                     ).then_inc(pool_step, 1)
                    pool.wait_ge(pool_step, i * 3 + (rows_base + 3))
                for c in range(4):
                    pool.wait_ge(mid_made, 4 * n + c + 1)
                    pool.tensor_tensor(pt[c][:, 2, :], r1[c % 2], pt[c][:, 1, :], ALU.subtract).then_inc(lo_made, 1)

            stage_a(pool, a)
            step[0] += 3 * NG
            pool.sem_inc(rows_made, 1)

            def normalise(n, g):
                pool.wait_ge(rec_made, NG * n + g + 1 + 1)
                if g == 0:
                    pool.wait_ge(pj_made, 2 * n + 2)
                pool.tensor_tensor(yn[:, g, :], ysb[:, g % 2, :], rec[:, g % 2, :], ALU.mult).then_inc(div_made, 1)

            def b(n, i, p):
                pool.wait_ge(xr_in[p], 16 * (i + 1))
                pool.tensor_tensor(xr[:, p], xr[:, p], bp[:, None, :].broadcast_to([P, TB, E]), ALU.add).then_inc(xr_made, 1)
                for g in range(NG):
                    if g >= 2:
                        normalise(n, g - 2)
                    for h in range(HG):
                        wait_apart(pool, exp_made, NSJ * (NG * n + g) + 3 * (h + 1) + 3)
                        v = pr_all[:, HG * (g % 2) + h, 0:W_R0].rearrange("p (t q) -> p t q", t=TB)
                        pool.affine_select(out=v, in_=v, compare_op=ALU.is_ge, fill=0.0, base=0,
                                           pattern=[[0, TB], [1, P]], channel_multiplier=-1).then_inc(sel_made, 1)
                normalise(n, 2)
                normalise(n, 3)

            pool.sem_inc(div_made, 2)
            pairs(pool, LOOPED // 2, b)
            pool.wait_ge(pos_made, 1)
            pool.wait_ge(list_init, 16)
            for p in range(2):
                pool.wait_ge(xnp_in[p], 16 * B // 2)
            for t in range(NT):
                pool.indirect_dma_start(out=xs_d, out_offset=bass.IndirectOffsetOnAxis(ap=pos[:, t:t + 1].bitcast(U32), axis=0),
                                        in_=xnp[:, t, :].bitcast(I32), in_offset=None).then_inc(scattered, 16)
            last_two(b)

            def tile_c(s, k, q):
                token = xs_sb[:, q, 2 * E:2 * E + 2].bitcast(U32)
                wait_apart(pool, xs_in[q], 16 * (k + 1))
                pool.indirect_dma_start(out=xg[:, q, :], out_offset=None, in_=xa_d,
                                        in_offset=bass.IndirectOffsetOnAxis(ap=token, axis=0),
                                        bounds_check=T - 1, oob_is_err=False).then_inc(xg_in[q], 16)

            def scatter_c(s, k, q):
                token = xs_sb[:, q, 2 * E:2 * E + 2].bitcast(U32)
                wait_apart(pool, ob_made, s + 1)
                pool.indirect_dma_start(out=out_rows, out_offset=bass.IndirectOffsetOnAxis(ap=token, axis=0),
                                        in_=ob[:, q, :], in_offset=None,
                                        bounds_check=T - 1, oob_is_err=False).then_inc(ob_out[q], 16)

            for p in range(2):
                pool.wait_ge(xa_out[p], 16 * B // 2)
            mark(pool.memset(xg[:, :, :], 0.0))
            with pool.Fori(0, TILES // 2) as k:
                for q in range(2):
                    tile_c(2 * k + q, k, q)
                for q in range(2):
                    scatter_c(2 * k + q, k, q)

        @block.scalar
        def _(act):
            act.sem_inc(exp_made, 3)
            act.sem_inc(y_copied, 1)
            act.wait_ge(cst_in, 160)
            act.activation(w_h[:, :, :], wk_f, ACT.Copy, scale=WS).then_inc(w_split, 1)
            act.activation(bqk[:, :], bqk[:, :], ACT.Copy, scale=WS).then_inc(act_step, 1)
            act.wait_ge(act_step, 1)

            def a(n, i, p):
                act.wait_ge(stats, n + 1)
                act.activation(std[:, :], mv[:, :, 1], ACT.Sqrt, bias=epst[:, 0:1]).then_inc(std_made, 1)
                act.wait_ge(t_made, n + 1)
                after(act, v_made, 4 * n - 4)
                for a_ in range(2):
                    act.activation(xt[p][:, a_].rearrange("p k n -> p (k n)"), bank[a_].bitcast(F16),
                                   ACT.Copy).then_inc(t_used, 1)
                act.wait_ge(we_in, 32 * (n + 1))
                after(act, we_out, 32 * n)
                act.activation(wsp[0], wst, ACT.Copy, scale=WS).then_inc(we_hi, 1)
                def hi(c):
                    act.wait_ge(qk_made, 4 * n + c + 1)
                    after(act, parts_out[c], 16 * PARTS * n)
                    act.activation(pt[c][:, 0, :], bank[2 + c], ACT.Identity, bias=bqk[:, c:c + 1]).then_inc(hi_made, 1)

                def mid(c):
                    act.wait_ge(r1_made, 4 * n + c + 1)
                    act.activation(pt[c][:, 1, :], r1[c % 2], ACT.Copy).then_inc(mid_made, 1)

                hi(0)
                for c in range(4):
                    if c < 3:
                        hi(c + 1)
                    mid(c)

            stage_a(act, a)

            act.wait_ge(q8, 2)
            act.activation(pe8[:, :, :], lg[:, :, :], ACT.Exp).then_inc(exp8, 1)

            def shift_rows(n1, p1):
                act.wait_ge(c_made, n1 + 1)
                for r in range(2):
                    act.dma_start(qs[R_SHIFT + r:R_SHIFT + r + 1, p1].rearrange("p g h n -> p (g h) n"),
                                  cc[:, p1, r, :]).then_inc(c_in[p1], 16)

            def copy_y(n, g):
                act.wait_ge(y_made, NG * n + g + 1 + 2)
                act.wait_ge(div_made, NG * n + g + 1)
                act.activation(ysb[:, g % 2, :], bank[5], ACT.Copy).then_inc(y_copied, 1)

            def b(n, i, p, more=True):
                for g in range(NG):
                    act.wait_ge(y_made, NG * n + g + 1)
                    for h in range(HG):
                        buf = pr_all[:, HG * (g % 2) + h, :]
                        for j, (c0, w) in enumerate(((W_R0, 384), (W_R1, 384), (W_DIAG, 512))):
                            act.wait_ge(s_made, NSJ * (NG * n + g) + 3 * h + j + 1)
                            act.activation(buf[:, c0:c0 + w], bank[2 + j][:, 0:w], ACT.Exp, scale=SCORE)\
                               .then_inc(exp_made, 1)
                            if g >= 1 and h == 3 and j == 1:
                                copy_y(n, g - 1)
                copy_y(n, NG - 1)
                if more:
                    shift_rows(n + 1, 1 - p)

            act.wait_ge(rows_in, 32)
            shift_rows(0, 0)
            pairs(act, LOOPED // 2, b)
            b(B - 2, B // 2 - 1, 0)
            b(B - 1, B // 2 - 1, 1, False)

            def gelu(s, q):
                act.wait_ge(h_made, s + 1)
                after(act, hl_made, s - 1)
                act.activation(hg[:, q, :], bank[2 + q], ACT.Gelu, scale=1.0 / WS).then_inc(hg_made, 1)
                act.wait_ge(hg_made, s + 1)
                after(act, o_made, s - 1)
                act.activation(hh[:, q, 0, :], hg[:, q, :], ACT.Copy).then_inc(hh_made, 1)

            gelu(0, 0)
            gelu(1, 1)
            with act.Fori(1, TILES // 2) as k:
                for q in range(2):
                    gelu(2 * k + q, q)

        @block.vector
        def _(dve):
            step = [0]

            def mark(ins):
                step[0] += 1
                ins.then_inc(dve_step, 1)
                dve.wait_ge(dve_step, step[0])

            dve.sem_inc(rec_made, 1)
            dve.sem_inc(xadd_made, 1)
            dve.wait_ge(w_split, 1)
            mark(dve.scalar_tensor_tensor(out=w_l[:, :, :], in0=wk_f, scalar=WS, in1=w_h[:, :, :],
                                          op0=ALU.mult, op1=ALU.subtract))
            dve.sem_inc(w_split, 1)
            mark(dve.tensor_scalar(sl[R_ALIBI:R_SHIFT, 1, :], sl[R_ALIBI:R_SHIFT, 0, :], 1.0 / SCORE, None, ALU.mult))
            al = slice(R_ALIBI, R_SHIFT)
            dve.wait_ge(const_made, 5)
            for r in range(3):
                mark(dve.tensor_copy(slb[al, r, :], sl[al, 1 + r, :]))
                if r < 2:
                    mark(dve.tensor_tensor(sl[al, 2 + r, :], sl[al, 1 + r, :], slb[al, r, :], ALU.subtract))
            mark(dve.tensor_scalar(sl[al, 4, :], slb[al, 0, :], idf[al, R_ALIBI:R_ALIBI + 1], None, ALU.mult))
            for r in (1, 2):
                mark(dve.scalar_tensor_tensor(out=sl[al, 4 + r, :], in0=slb[al, r, :],
                                              scalar=idf[al, R_ALIBI + r:R_ALIBI + r + 1],
                                              in1=sl[al, 3 + r, :], op0=ALU.mult, op1=ALU.add))
            dve.sem_inc(q8, 1)
            mark0 = step[0]
            A_STEPS = 4

            def a(n, i, p):
                def link(ins, k):
                    ins.then_inc(dve_step, 1)
                    dve.wait_ge(dve_step, mark0 + n * A_STEPS + k)

                dve.wait_ge(x_in[p], 16 * (i + 1))
                for t in range(TB):
                    last = dve.bn_stats(bst[:, t, :], xin[p][:, t, :])
                last.then_inc(dve_step, 1)
                wait_apart(dve, dve_step, mark0 + n * A_STEPS + 1)
                for t in range(TB):
                    last = dve.bn_aggr(mv[:, t, :], bst[:, t, :])
                last.then_inc(stats, 1)
                dve.wait_ge(std_made, n + 1)
                link(dve.reciprocal(rstd[:, :], std[:, :]), 2)
                after(dve, xw_made, n)
                for t in range(TB):
                    last = dve.tensor_scalar(xn[:, t, :], xin[p][:, t, :], mv[:, t, 0:1], rstd[:, t:t + 1],
                                             ALU.subtract, ALU.mult)
                link(last, 3)
                dve.sem_inc(x_made, 1)
                after(dve, t_made, n - 1)
                after(dve, xnp_in[p], 16 * i)
                link(dve.tensor_copy(xw[p][:, :, 0:E], xn), 4)
                dve.tensor_tensor(xw[p][:, :, E:2 * E], xn, xw[p][:, :, 0:E], ALU.subtract).then_inc(xw_made, 1)
                dve.wait_ge(we_hi, n + 1)
                dve.scalar_tensor_tensor(out=wsp[1], in0=wst, scalar=WS, in1=wsp[0], op0=ALU.mult,
                                         op1=ALU.subtract).then_inc(we_lo, 1)
                for c in range(4):
                    dve.wait_ge(hi_made, 4 * n + c + 1)
                    after(dve, lo_made, 4 * n + c - 1)
                    dve.scalar_tensor_tensor(out=r1[c % 2], in0=bank[2 + c], scalar=bqk[:, c:c + 1],
                                             in1=pt[c][:, 0, :], op0=ALU.add, op1=ALU.subtract).then_inc(r1_made, 1)
                after(dve, v_out[p], 16 * i)
                for t in range(TB):
                    dve.wait_ge(v_made, 4 * n + t + 1)
                    vb = bank[6 + t % 2]
                    dve.scalar_tensor_tensor(out=vt[:, p, t, :, 0:D], in0=vb[:, 0:E].rearrange("p (h d) -> p h d", h=H),
                                             scalar=1.0 / WS, in1=bv[:, :, :], op0=ALU.mult, op1=ALU.add)
                    dve.tensor_scalar(lg[:, bass.ds(4 * n + t, 1), :].rearrange("p a b -> p (a b)"), vb[:, E:E + X],
                                      1.0 / WS, None, ALU.mult).then_inc(v_used, 1)

            stage_a(dve, a)
            step[0] += A_STEPS * B

            dve.wait_ge(v_used, NT)
            dve.wait_ge(consts, 1)
            bc = lambda ap: ap[:, :, None].broadcast_to([P, NT, X])
            mark(dve.tensor_reduce(r32[:, 0, :], lg[:, :, :], AX, ALU.max))
            mark(dve.tensor_tensor(lg[:, :, :], lg[:, :, :], bc(r32[:, 0, :]), ALU.subtract))
            dve.sem_inc(q8, 1)
            dve.memset(bank[5], 0.0).then_inc(y_copied, 1)
            dve.wait_ge(exp8, 1)
            mark(dve.tensor_reduce(r32[:, 1, :], pe8[:, :, :], AX, ALU.add))
            mark(dve.reciprocal(r32[:, 2, :], r32[:, 1, :]))
            mark(dve.tensor_tensor(pr[:, :, :].rearrange("p e t -> p t e"), pe8[:, :, :], bc(r32[:, 2, :]), ALU.mult))

            def row_max(n1, p1, g, k):
                u = NU * (NG * n1 + g) + k
                qt, hs = UNITS[k]
                w = (qt + 1) * P
                dve.wait_ge(sm_made, u + 1)
                src = bank[(NU * g + k) % 2][:, 0:w * len(hs)].rearrange("p (h c) -> p h c", c=w)
                h0 = g * HG + hs[0]
                dve.tensor_reduce(mx[:, p1, qt, h0:h0 + len(hs)], src, AX, ALU.max).then_inc(max_made, 1)

            def make_shift(n1, p1):
                dve.wait_ge(ct_made, n1 + 1)
                dve.tensor_scalar(cc[:, p1, 0, :], bank[7][0:H, :], -1.0, None, ALU.mult).then_inc(shift_step, 1)
                dve.wait_ge(shift_step, n1 + 1)
                dve.scalar_tensor_tensor(out=cc[:, p1, 1, :], in0=bank[7][0:H, :], scalar=-1.0, in1=cc[:, p1, 0, :],
                                         op0=ALU.mult, op1=ALU.subtract).then_inc(c_made, 1)

            def divide(n, g):
                dve.wait_ge(sum_made, NG * n + g + 1)
                dve.wait_ge(div_made, NG * n + g + 1)
                dve.reciprocal(rec[:, g % 2, :], bank[6]).then_inc(rec_made, 1)

            def residual(n, p, j):
                if j == 0:
                    dve.wait_ge(xr_made, n + 1)
                dve.wait_ge(pj_made, 2 * n + j + 1 + 2)
                v = xr[:, p, 2 * j:2 * j + 2, :]
                dve.tensor_tensor(v, bank[7].rearrange("p (t e) -> p t e", t=2), v, ALU.add).then_inc(xadd_made, 1)

            bisect_base = step[0]

            def bisect_count(it):
                k0 = bisect_base + 4 * it
                dve.tensor_tensor(cand[:, :].bitcast(U32), thr[:, :].bitcast(U32),
                                  bits[:, bass.ds(it, 1), :].rearrange("p a e -> p (a e)"),
                                  ALU.bitwise_or).then_inc(dve_step, 1)
                dve.wait_ge(dve_step, k0 + 1)
                dve.tensor_tensor(hit[:, :, :], pr[:, :, :], cand[:, :, None].broadcast_to([P, X, NT]),
                                  ALU.is_ge).then_inc(dve_step, 1)
                dve.wait_ge(dve_step, k0 + 2)
                with nc.allow_low_precision("counts up to 32 are exact"):
                    dve.tensor_reduce(cnt[:, :], hit[:, :, :], AX, ALU.add).then_inc(cnt_made, 1)

            def bisect_take(it):
                k0 = bisect_base + 4 * it
                dve.wait_ge(tot_made, it + 1)
                dve.tensor_scalar(acc[:, :], bank[7][:, 0:X], float(CAP), None, ALU.is_ge).then_inc(dve_step, 1)
                wait_apart(dve, dve_step, k0 + 3)
                dve.copy_predicated(thr[:, :], acc[:, :], cand[:, :]).then_inc(dve_step, 1)
                dve.wait_ge(dve_step, k0 + 4)

            for g in range(NG):
                for k in range(NU):
                    row_max(0, 0, g, k)
            make_shift(0, 0)

            def b(n, i, p, more=True, bis=True):
                for g in range(NG):
                    it = n * BPB + sum(BIS[:g])
                    if bis:
                        bisect_count(it)
                    for k in range(NU):
                        if more:
                            row_max(n + 1, 1 - p, g, k)
                        if k == 3 and g >= 2:
                            divide(n, g - 2)
                        if bis and k == 4:
                            bisect_take(it)
                            if BIS[g] == 2:
                                bisect_count(it + 1)
                        if bis and k == 9 and BIS[g] == 2:
                            bisect_take(it + 1)
                divide(n, 2)
                if more:
                    make_shift(n + 1, 1 - p)
                divide(n, 3)
                for j in range(2):
                    residual(n, p, j)

            pairs(dve, LOOPED // 2, b)
            step[0] += 4 * BPB * LOOPED

            e8 = lambda ap: ap[:, :, None].broadcast_to([P, X, NT])
            t32 = lambda ap: ap[:, None, :].broadcast_to([P, X, NT])
            by_t = lambda ap: ap[:, :, :].rearrange("p e t -> p t e")
            TT = lambda *a, **k: mark(dve.tensor_tensor(*a, **k))

            def offsets(dst, k):
                dve.wait_ge(rt_pe, k)
                mark(dve.tensor_copy(rr[2][:, :, :], bank[6][:, 256:512].rearrange("p (e t) -> p e t", e=X)))
                fl = lambda a_: a_[:, :, :].rearrange("p e t -> p (e t)")
                mark(dve.tensor_tensor_scan(fl(dst), fl(seg), fl(rr[2]), 0.0, ALU.mult, ALU.add))
                mark(dve.tensor_copy(r8[:, 2, :], dst[:, :, NT - 1]))
                TT(dst[:, :, :], dst[:, :, :], rr[2][:, :, :], ALU.subtract)
                TT(dst[:, :, :], bank[6][:, 0:256].rearrange("p (e t) -> p e t", e=X), dst[:, :, :], ALU.add)

            TT(gtb[:, :, :], pr[:, :, :], e8(thr), ALU.is_gt)
            with nc.allow_low_precision("counts up to 32 are exact"):
                mark(dve.tensor_reduce(cnt[:, :], gtb[:, :, :], AX, ALU.add))
            TT(hit[:, :, :], pr[:, :, :], e8(thr), ALU.is_equal)
            dve.sem_inc(rt_dve, 1)
            offsets(rr[0], 1)
            mark(dve.tensor_scalar(r8[:, 0, :], bank[7][:, 0:X], -1.0, float(CAP), ALU.mult, ALU.add))
            TT(rr[0][:, :, :], rr[0][:, :, :], e8(r8[:, 0, :]), ALU.is_lt)
            TT(rr[0][:, :, :], rr[0][:, :, :], hit[:, :, :], ALU.mult)
            TT(rr[0][:, :, :], rr[0][:, :, :], gtb[:, :, :], ALU.max)
            mark(dve.tensor_reduce(r32[:, 0, :], by_t(rr[0]), AX, ALU.max))
            TT(rr[0][:, :, :], rr[0][:, :, :], t32(r32[:, 0, :]), ALU.is_ge)
            TT(rr[1][:, :, :], rr[0][:, :, :], pr[:, :, :], ALU.mult)
            mark(dve.scalar_tensor_tensor(out=rr[1][:, :, :], in0=rr[0][:, :, :], scalar=-1.0, in1=rr[1][:, :, :],
                                          op0=ALU.add, op1=ALU.add))
            mark(dve.tensor_reduce(r32[:, 1, :], by_t(rr[1]), AX, ALU.max))
            TT(rr[1][:, :, :], rr[1][:, :, :], t32(r32[:, 1, :]), ALU.is_equal)
            TT(rr[1][:, :, :], rr[1][:, :, :], rank8[:, :, :], ALU.mult)
            mark(dve.tensor_reduce(r32[:, 2, :], by_t(rr[1]), AX, ALU.max))
            TT(hit[:, :, :], rr[1][:, :, :], t32(r32[:, 2, :]), ALU.is_equal)
            dve.sem_inc(rt_dve, 1)
            TT(rr[1][:, :, :], hit[:, :, :], pr[:, :, :], ALU.mult)
            mark(dve.tensor_reduce(r32[:, 3, :], by_t(rr[1]), AX, ALU.max))
            mark(dve.tensor_scalar(r32[:, 3, :], r32[:, 3, :], 1.0 / WS, None, ALU.mult))
            offsets(rr[0], 2)
            TT(rr[1][:, :, :], e8(r8[:, 2, :]), lim[:, :, :], ALU.is_gt)
            mark(dve.tensor_reduce(r8[:, 3, :], rr[1][:, :, :], AX, ALU.add))
            mark(dve.memset(r8[:, 0, :], 1.0))
            mark(dve.tensor_tensor_scan(r8[:, 4, :], r8[:, 0, :], r8[:, 3, :], 0.0, ALU.mult, ALU.add))
            TT(r8[:, 5, :], r8[:, 4, :], r8[:, 3, :], ALU.subtract)
            mark(dve.tensor_scalar(r8[:, 5, :], r8[:, 5, :], float(P), None, ALU.mult))
            TT(rr[0][:, :, :], rr[0][:, :, :], e8(r8[:, 5, :]), ALU.add)
            TT(rr[0][:, :, :], rr[0][:, :, :], hit[:, :, :], ALU.mult)
            mark(dve.tensor_reduce(r32[:, 4, :], by_t(rr[0]), AX, ALU.add))
            mark(dve.tensor_copy(pos[:, :], r32[:, 4, :]))
            for p in range(2):
                dve.wait_ge(xnp_in[p], 16 * B // 2)
            mark(dve.tensor_copy(xnp[:, :, 2 * E:2 * E + 2].bitcast(I32).rearrange("p t a -> p (t a)"), tok[:, :]))
            mark(dve.tensor_copy(xnp[:, :, 2 * E + 2:].bitcast(F32).rearrange("p t a -> p (t a)"), r32[:, 3, :]))
            dve.sem_inc(pos_made, 1)
            TT(ecmp[:, :, :], r8[:, 4, :][:, None, :].broadcast_to([P, TILES, X]), sno[:, :, :], ALU.is_le)
            mark(dve.tensor_reduce(eidf[:, :], ecmp[:, :, :], AX, ALU.add))
            mark(dve.tensor_scalar(eid[:, :], eidf[:, :], float(X - 1), None, ALU.min))
            dve.sem_inc(pos_made, 1)

            b(B - 2, B // 2 - 1, 0, True, False)
            b(B - 1, B // 2 - 1, 1, False, False)

            def take_x(s, q):
                dve.wait_ge(tt_made, s + 1)
                dve.tensor_copy(xT[:, q].rearrange("p a n -> p (a n)"), bank[q].bitcast(F16)[:, 0:512]).then_inc(xT_made, 1)

            def low(s, q):
                dve.wait_ge(hh_made, s + 1)
                dve.tensor_tensor(hh[:, q, 1, :], hg[:, q, :], hh[:, q, 0, :], ALU.subtract).then_inc(hl_made, 1)

            def combine(s, k, q):
                dve.wait_ge(o_made, s + 1)
                dve.wait_ge(xg_in[q], 16 * (k + 1))
                after(dve, ob_out[q], 16 * k)
                dve.scalar_tensor_tensor(out=ob[:, q, :], in0=bank[4 + q][:, 0:E],
                                         scalar=xs_sb[:, q, 2 * E + 2:].bitcast(F32), in1=xg[:, q, :],
                                         op0=ALU.mult, op1=ALU.add).then_inc(ob_made, 1)

            def two_tiles(k):
                combine(2 * k, k, 0)
                take_x(2 * k + 2, 0)
                low(2 * k + 1, 1)
                combine(2 * k + 1, k, 1)
                take_x(2 * k + 3, 1)
                low(2 * k + 2, 0)

            take_x(0, 0)
            take_x(1, 1)
            low(0, 0)
            two_tiles(0)
            with dve.Fori(1, TILES // 2 - 1) as k:
                two_tiles(k)
            combine(TILES - 2, TILES // 2 - 1, 0)
            low(TILES - 1, 1)
            combine(TILES - 1, TILES // 2 - 1, 1)

        @block.tensor
        def _(pe):
            pe.sem_inc(y_made, 2)
            pe.sem_inc(pj_made, 2)
            pe.wait_ge(const_made, 12)
            pe.wait_ge(w_split, 2)

            def six(out, lhs, rhs):
                terms = [(0, 0), (0, 1), (1, 0)]
                for k in range(EC):
                    for j, (a_, b_) in enumerate(terms):
                        last = pe.matmul(out, lhs(a_, k), rhs(b_, k), start=(k == 0 and j == 0),
                                         stop=(k == EC - 1 and j == 2))
                return last

            def a(n, i, p):
                pe.wait_ge(xw_made, n + 1)
                after(pe, t_used, 2 * n)
                for t in range(TB):
                    for a_ in range(2):
                        for k in range(EC):
                            last = pe.transpose(bank[a_].bitcast(F16)[:, k * S + t * P:k * S + (t + 1) * P],
                                                xw[p][:, t, (a_ * EC + k) * P:(a_ * EC + k + 1) * P], id16[:, :])
                last.then_inc(t_made, 1)
                pe.wait_ge(t_used, 2 * n + 2)
                W = (w_h, w_l)
                for c in range(4):
                    after(pe, r1_made, 4 * n + c - 3)
                    six(bank[2 + c], lambda a_, k: W[a_][:, k, c * P:(c + 1) * P],
                        lambda b_, k: xt[p][:, b_, k, :]).then_inc(qk_made, 1)
                for t in range(TB):
                    after(pe, v_used, 4 * n + t - 1)
                    last = six(bank[6 + t % 2][:, 0:E + X], lambda a_, k: xt[p][:, a_, k, t * P:(t + 1) * P],
                               lambda b_, k: W[b_][:, k, 2 * E:3 * E + X])
                    last.then_inc(v_made, 1)

            stage_a(pe, a)
            pe.wait_ge(r1_made, 4 * B)
            pe.wait_ge(v_used, 4 * B)
            pe.wait_ge(y_copied, 2)

            def max_unit(n1, p1, i1, g, k):
                u = NU * (NG * n1 + g) + k
                if k == 0:
                    pe.wait_ge(grp_in[p1][g], 16 * 12 * (i1 + 1))
                if not isinstance(n1, int) or u >= 2:
                    pe.wait_ge(max_made, u - 1)
                qt, hs = UNITS[k]
                w = (qt + 1) * P
                dst = bank[(NU * g + k) % 2]
                for j, h in enumerate(hs):
                    pe.matmul(dst[:, j * w:(j + 1) * w], qs[0:R_SHIFT, p1, g, h, qt * P:w],
                              ks[0:R_SHIFT, p1, g, h, 0:w], start=True, stop=False)
                    last = pe.matmul(dst[:, (j + 1) * w - P:(j + 1) * w], idb[:, :], maxmask[:, :],
                                     start=False, stop=True)
                last.then_inc(sm_made, 1)

            def scores(n, p, i, g, h, j):
                v = NSJ * (NG * n + g) + 3 * h + j
                if g == 0 and h == 0 and j == 0:
                    pe.wait_ge(c_in[p], 32 * (i + 1))
                pe.wait_ge(exp_made, v + 1)
                blocks = ([(0, P, 384, 0)], [(1, 2 * P, 256, 0), (2, 3 * P, P, 256)],
                          [(t, t * P, P, t * P) for t in range(TB)])[j]
                for t, q0, w, c0 in blocks:
                    last = pe.matmul(bank[2 + j][:, c0:c0 + w], ks[:, p, g, h, t * P:(t + 1) * P],
                                     qs[:, p, g, h, q0:q0 + w], start=True, stop=True)
                last.then_inc(s_made, 1)

            def with_v(n, p, i, g, k):
                if k == 0:
                    pe.wait_ge(sel_made, HG * (NG * n + g + 1))
                    pe.wait_ge(exp_made, NSJ * (NG * n + g + 1) + 3)
                    pe.wait_ge(y_copied, NG * n + g + 2)
                    if g == 0:
                        pe.wait_ge(vb_in[p], 16 * (i + 1))
                t, c0, q0, w = PIECES[k]
                for h in range(HG):
                    last = pe.matmul(bank[5][32 * h:32 * h + VW, q0:q0 + w], vt[:, p, t, g * HG + h, :],
                                     pr_all[:, HG * (g % 2) + h, c0:c0 + w], start=(k == 0),
                                     stop=(k == len(PIECES) - 1), skip_group_check=True)
                if k == len(PIECES) - 1:
                    last.then_inc(y_made, 1)

            def sums(n, g):
                pe.wait_ge(y_copied, NG * n + g + 3)
                pe.wait_ge(rec_made, NG * n + g + 1)
                pe.matmul(bank[6], spread[:, :], ysb[:, g % 2, :], start=True, stop=True).then_inc(sum_made, 1)

            def turn_max(n1, p1):
                pe.wait_ge(max_made, NU * NG * (n1 + 1))
                for t in range(TB):
                    last = pe.transpose(bank[7][0:H, t * P:(t + 1) * P], mx[:, p1, t, :], idf[:, :])
                last.then_inc(ct_made, 1)

            def project(n, j):
                if j == 0:
                    pe.wait_ge(div_made, NG * (n + 1) + 2)
                else:
                    pe.wait_ge(xadd_made, 2 * n + 1 + 1)
                for t in range(2):
                    for g in range(NG):
                        last = pe.matmul(bank[7][:, t * E:(t + 1) * E], yn[:, g, (2 * j + t) * P:(2 * j + t + 1) * P],
                                         wp[:, g, :], start=(g == 0), stop=(g == NG - 1))
                last.then_inc(pj_made, 1)

            def total(it):
                pe.wait_ge(cnt_made, it + 1)
                pe.matmul(bank[7][:, 0:X], ones[:, :], cnt[:, :], start=True, stop=True).then_inc(tot_made, 1)

            for g in range(NG):
                for k in range(NU):
                    max_unit(0, 0, 0, g, k)
            turn_max(0, 0)
            pe.wait_ge(c_made, 1)

            def b(n, i, p, more=True, bis=True):
                for g in range(NG):
                    it = n * BPB + sum(BIS[:g])
                    for k in range(NSJ):
                        if more and k < NU:
                            max_unit(n + 1, 1 - p, i + p, g, k)
                        scores(n, p, i, g, k // 3, k % 3)
                        if k == 2 and g >= 2:
                            sums(n, g - 2)
                        if bis and k == 3:
                            total(it)
                        if bis and k == 8 and BIS[g] == 2:
                            total(it + 1)
                        if g >= 1 and 4 <= k <= 10:
                            with_v(n, p, i, g - 1, k - 4)
                sums(n, 2)
                for k in range(len(PIECES)):
                    with_v(n, p, i, 3, k)
                if more:
                    pe.wait_ge(xadd_made, 2 * n + 1)
                    turn_max(n + 1, 1 - p)
                sums(n, 3)
                if more:
                    pe.wait_ge(c_made, n + 2)
                for j in range(2):
                    project(n, j)

            pairs(pe, LOOPED // 2, b)

            def count_marks(k):
                pe.wait_ge(rt_dve, k)
                v = hit[:, :, :].rearrange("p e t -> p (e t)")
                pe.matmul(bank[6][:, 0:256], tri[:, :], v, start=True, stop=True)
                last = pe.matmul(bank[6][:, 256:512], ones[:, :], v, start=True, stop=True)
                if k == 1:
                    last = pe.matmul(bank[7][:, 0:X], ones[:, :], cnt[:, :], start=True, stop=True)
                last.then_inc(rt_pe, 1)

            pe.wait_ge(rec_made, NG * LOOPED + 1)
            pe.wait_ge(xadd_made, 2 * LOOPED + 1)
            count_marks(1)
            count_marks(2)
            pe.wait_ge(pos_made, 1)
            b(B - 2, B // 2 - 1, 0, True, False)
            b(B - 1, B // 2 - 1, 1, False, False)

            def turn_x(s, k, q):
                pe.wait_ge(xs_in[q], 16 * (k + 1))
                for j in range(4):
                    last = pe.transpose(bank[q].bitcast(F16)[:, j * P:(j + 1) * P], xs_sb[:, q, j * P:(j + 1) * P], id16[:, :])
                last.then_inc(tt_made, 1)

            def expert_of(s):
                return pe.value_load(eid[0:1, bass.ds(s, 1)], min_val=0, max_val=X - 1)

            def up(s, q, e):
                pe.wait_ge(xT_made, s + 1)
                after(pe, hg_made, s - 1)
                terms = [(0, 0), (0, 1), (1, 0)]
                for f in range(FC):
                    for k in range(EC):
                        for j, (a_, b_) in enumerate(terms):
                            c0 = k * FF + f * P
                            last = pe.matmul(bank[2 + q][:, f * P:(f + 1) * P],
                                             w1_sb[:, bass.ds(e, 1), a_, c0:c0 + P].rearrange("p x w -> p (x w)"),
                                             xT[:, q, b_ * EC + k, :], start=(k == 0 and j == 0),
                                             stop=(k == EC - 1 and j == 2))
                last.then_inc(h_made, 1)

            def down(s, q, e):
                pe.wait_ge(hl_made, s + 1)
                after(pe, ob_made, s - 1)
                w2p = (w2_h, w2_l)
                for f in range(FC):
                    for j, (a_, b_) in enumerate([(0, 0), (0, 1), (1, 0)]):
                        last = pe.matmul(bank[4 + q][:, 0:E], hh[:, q, a_, f * P:(f + 1) * P],
                                         w2p[b_][:, bass.ds(e, 1), f * E:(f + 1) * E].rearrange("p x w -> p (x w)"),
                                         start=(f == 0 and j == 0), stop=(f == FC - 1 and j == 2))
                last.then_inc(o_made, 1)

            pe.wait_ge(w1_in, 32)
            pe.wait_ge(w2_in, 32)
            pe.wait_ge(pos_made, 2)
            turn_x(0, 0, 0)
            up(0, 0, expert_of(0))
            turn_x(1, 0, 1)
            up(1, 1, expert_of(1))
            def two_tiles(k):
                s = 2 * k
                down(s, 0, expert_of(s))
                turn_x(s + 2, k + 1, 0)
                up(s + 2, 0, expert_of(s + 2))
                down(s + 1, 1, expert_of(s + 1))
                turn_x(s + 3, k + 1, 1)
                up(s + 3, 1, expert_of(s + 3))

            two_tiles(0)
            with pe.Fori(1, TILES // 2 - 1) as k:
                two_tiles(k)
            down(TILES - 2, 0, expert_of(TILES - 2))
            down(TILES - 1, 1, expert_of(TILES - 1))


_INS = ['L0_attn_x', 'L0_attn_W_kqv', 'L0_attn_b_kqv', 'L0_attn_W_proj', 'L0_attn_b_proj', 'L0_attn_slopes',
        'L0_ffn_Wg', 'L0_ffn_W1', 'L0_ffn_W2']


def kernel(**inputs):
    import numpy as _np
    import concourse.bacc as _bacc
    from concourse import mybir as _mybir
    from concourse.bass_utils import run_bass_kernel_spmd as _run

    nc = _bacc.Bacc("TRN2", target_bir_lowering=False, num_devices=1)
    arrays, args = {}, []
    for name in _INS:
        a = _np.ascontiguousarray(inputs[name])
        arrays[f"in_{name}_dram"] = a
        args.append(nc.dram_tensor(f"in_{name}_dram", a.shape, _mybir.dt.from_np(a.dtype), kind="ExternalInput").ap())
    args.append(nc.dram_tensor("out_0_dram", (B, S, E), _mybir.dt.float32, kind="ExternalOutput").ap())
    layer(nc, *args)
    r = _run(nc, [arrays], core_ids=[0])
    return r.results[0]["out_0_dram"]
```

```python
from contextlib import ExitStack

import concourse.bass as bass
from concourse import mybir

F32, F16, BF16 = mybir.dt.float32, mybir.dt.float16, mybir.dt.bfloat16
I32, U32 = mybir.dt.int32, mybir.dt.uint32
ALU = mybir.AluOpType
ACT = mybir.ActivationFunctionType
AX = mybir.AxisListType.X

P = 128
B, S, E, H, D = 8, 512, 256, 16, 16
T = B * S
NT = T // P
TB = S // P
EC = E // P
X, FF = 8, 512
FC = FF // P
CAP = T // X
TILES = NT + X
HG = 4
NG = H // HG
WS = 256.0
SCORE = 1.0 / (4.0 * WS * WS)
NEG = -1e30 / SCORE
EPS = 1e-5
PARTS = 3
Q_ROWS = (0, 0, 0, 1, 1, 2)
K_ROWS = (0, 1, 2, 0, 1, 0)
R_ALIBI = len(Q_ROWS) * D
R_SHIFT = R_ALIBI + 3
R_FAR = R_SHIFT + 2
FAR = -(-S // (P - R_FAR + 1))
MID = 256
VW = D + 1
ROW = 2 * E + 4
BITS = 30
BIS = (2, 1, 2, 1)
BPB = sum(BIS)
LOOPED = 6
NO_TOKEN = 1 << 20
UNITS = [(3, (h,)) for h in range(4)] + [(2, (h,)) for h in range(4)] + \
        [(1, (0, 1)), (1, (2, 3)), (0, (0, 1, 2, 3))]
NU = len(UNITS)
NSJ = 3 * HG
TURN = NU * NG + 1
W_DIAG, W_R0, W_R1, W_R2 = 0, 512, 896, 1152
W_ALL = 1280
PIECES = [(0, W_R0, 128, 384), (0, 0, 0, 128), (1, W_R1, 256, 256), (2, W_R2, 384, 128),
          (1, 128, 128, 128), (2, 256, 256, 128), (3, 384, 384, 128)]


def layer(nc, x, w_kqv, b_kqv, w_proj, b_proj, slopes, wg, w1, w2, out):
    x_t = x.rearrange("b (t p) e -> b p t e", p=P)
    qk_d = [nc.dram_tensor(f"{n}_parts", [PARTS, H * D, T], BF16, kind="Internal").ap() for n in "kq"]
    v_d = nc.dram_tensor("v_rows", [B, P, TB * H * VW], F32, kind="Internal").ap()
    xa_d = nc.dram_tensor("x_plus_attention", [T, E], F32, kind="Internal").ap()
    ws_d = nc.dram_tensor("expert_parts", [X, P, 2, 2, 1024], F16, kind="Internal").ap()
    xs_d = nc.dram_tensor("sorted_rows", [TILES * P, ROW // 2], I32, kind="Internal").ap()
    out_rows = out.rearrange("b s e -> (b s) e")
    xa_t = xa_d.rearrange("(b t p) e -> b p t e", p=P, t=TB)

    with ExitStack() as ctx:
        def sb(name, shape, dt):
            return ctx.enter_context(nc.sbuf_tensor(name, shape, dt))

        def sem(name):
            return ctx.enter_context(nc.semaphore(name))

        def sems(name, n=2):
            return [sem(f"{name}{i}") for i in range(n)]

        ps = ctx.enter_context(nc.psum_tensor("ps", [P, 8, 512], F32))
        bank = [ps[:, i, :] for i in range(8)]

        id16 = sb("id16", [P, P], F16)
        idb = sb("idb", [P, P], BF16)
        idf = sb("idf", [P, P], F32)
        ones = sb("ones", [P, P], BF16)
        tri = sb("tri", [P, P], BF16)
        maxmask = sb("maxmask", [P, P], BF16)
        bits = sb("bits", [P, LOOPED * BPB, X], U32)
        epst = sb("epst", [P, 1], F32)
        seg = sb("seg", [P, X, NT], F32)
        rank8 = sb("rank8", [P, X, NT], F32)
        lim = sb("lim", [P, X, NT], F32)
        sno = sb("sno", [P, TILES, X], F32)
        iot = sb("iot", [P, TILES * X], I32)
        tok = sb("tok", [P, NT], I32)
        w_h = sb("w_h", [P, EC, 3 * E + X], F16)
        w_l = sb("w_l", [P, EC, 3 * E + X], F16)
        bqk = sb("bqk", [P, 4], F32)
        bv = sb("bv", [P, H, D], F32)
        bp = sb("bp", [P, E], F32)
        wp = sb("wp", [P, NG, E], F32)
        sl = sb("sl", [P, 7, H], F32)
        slb = sb("slb", [P, 3, H], BF16)
        qs = sb("qs", [P, 2, NG, HG, S], BF16)
        ks = sb("ks", [P, 2, NG, HG, S], BF16)
        pr_all = sb("pr_all", [P, 8, W_ALL], F32)
        vt = sb("vt", [P, 2, TB, H, VW], F32)
        xnp = sb("xnp", [P, NT, ROW], F16)
        ysb = sb("ysb", [P, 2, S], F32)
        yt = sb("yt", [P, S // 32, 32], F32)
        rec = sb("rec", [P, S // 32], F32)
        rec_wide = sb("rec_wide", [P, 2, S], F32)
        yn = sb("yn", [P, NG, S], F32)
        xr = sb("xr", [P, 2, TB, E], F32)
        mx = sb("mx", [P, 2, TB, H], F32)
        cc = sb("cc", [H, 2, 2, S], BF16)
        lg = sb("lg", [P, NT, X], F32)
        pe8 = sb("pe8", [P, NT, X], F32)
        pr = sb("pr", [P, X, NT], F32)
        thr = sb("thr", [P, X], F32)
        cand = sb("cand", [P, X], F32)
        hit = sb("hit", [P, X, NT], BF16)
        cnt = sb("cnt", [P, X], BF16)
        acc = sb("acc", [P, X], U32)
        r32 = sb("r32", [P, 6, NT], F32)
        r8 = sb("r8", [P, 6, X], F32)
        rr = [sb(f"rr{i}", [P, X, NT], F32) for i in range(3)]
        gtb = sb("gtb", [P, X, NT], BF16)
        pos = sb("pos", [P, NT], I32)
        ecmp = sb("ecmp", [P, TILES, X], F32)
        eidf = sb("eidf", [P, TILES], F32)
        eid = sb("eid", [P, TILES], I32)

        posi = rec_wide[:, 0, :].bitcast(I32)
        k_rows = ysb[:, 0, :].bitcast(BF16)[:, 0:S]
        q_rows = ysb[:, 1, :].bitcast(BF16)[:, 0:S]

        flat = pr_all[:, :, :].rearrange("p a b -> p (a b)")
        at = [0]

        def cut(n_bytes, dt, pattern=None, **dims):
            n = n_bytes // 4
            v = flat[:, at[0]:at[0] + n]
            at[0] += n
            assert at[0] <= 8 * W_ALL
            v = v if dt == F32 else v.bitcast(dt)
            return v.rearrange(pattern, **dims) if pattern else v

        xin = [cut(4096, F32, "p (t e) -> p t e", t=TB) for _ in range(2)]
        xn = cut(4096, F32, "p (t e) -> p t e", t=TB)
        xw = [cut(4096, F16, "p (t e) -> p t e", t=TB) for _ in range(2)]
        xt = [cut(4096, F16, "p (a k n) -> p a k n", a=2, k=EC) for _ in range(2)]
        r1 = [cut(2048, F32) for _ in range(2)]
        bst = sb("bst", [P, TB, 6], F32)
        mv = sb("mv", [P, TB, 2], F32)
        std = sb("std", [P, TB], F32)
        rstd = sb("rstd", [P, TB], F32)
        pt = [ks[:, 1, c, 0:PARTS, :] for c in range(4)]
        wst = qs[:, 1, 0:2, :, :].rearrange("p a b c -> p (a b c)").bitcast(F32)
        wsp = [qs[:, 1, 2 + j, :, :].rearrange("p b c -> p (b c)").bitcast(F16) for j in range(2)]
        wk_f = qs[:, 0, 0:2, :, :].rearrange("p a b c -> p (a b c)").bitcast(F32)[:, 0:EC * (3 * E + X)] \
            .rearrange("p (k c) -> p k c", k=EC)

        w1_sb = xnp[:, :, :].rearrange("p a b -> p (a b)")[:, 0:X * 2 * 1024] \
            .rearrange("p (x a w) -> p x a w", x=X, a=2)
        w2_h = qs[:, 0, :, :, :].rearrange("p a b c -> p (a b c)").bitcast(F16) \
            .rearrange("p (x w) -> p x w", x=X)
        w2_l = ks[:, 0, :, :, :].rearrange("p a b c -> p (a b c)").bitcast(F16) \
            .rearrange("p (x w) -> p x w", x=X)
        at[0] = 0
        xs_sb = cut(8 * ROW * 2, F16, "p (q c) -> p q c", q=8)
        xT = cut(2 * 4 * P * 2, F16, "p (q a c) -> p q a c", q=2, a=4)
        hg = cut(2 * FF * 4, F32, "p (q c) -> p q c", q=2)
        hh = cut(2 * 2 * FF * 2, F16, "p (q a c) -> p q a c", q=2, a=2)
        xg = cut(8 * E * 4, F32, "p (q c) -> p q c", q=8)
        ob = cut(8 * E * 4, F32, "p (q c) -> p q c", q=8)
        empty = sb("empty", [P, ROW], F16)

        const_made = sem("const_made")
        pool_step = sem("pool_step")
        cst_in = sem("cst_in")
        dve_step = sem("dve_step")
        act_step = sem("act_step")
        w_split = sem("w_split")
        x_in, x_made = sems("x_in"), sem("x_made")
        stats = sem("stats")
        std_made = sem("std_made")
        xw_made = sem("xw_made")
        xnp_in = sems("xnp_in")
        t_made, t_used = sem("t_made"), sem("t_used")
        qk_made, hi_made, r1_made, mid_made, lo_made = (sem(n) for n in ("qk_made", "hi_made", "r1_made", "mid_made", "lo_made"))
        parts_out = sems("parts_out", 4)
        v_made, v_used = sem("v_made"), sem("v_used")
        v_out = sems("v_out")
        we_in, we_hi, we_lo, we_out = sem("we_in"), sem("we_hi"), sem("we_lo"), sem("we_out")
        q8 = sem("q8")
        rows_made, rows_in = sem("rows_made"), sem("rows_in")
        exp8 = sem("exp8")
        grp_in = [sems(f"grp_in{p}_", NG) for p in range(2)]
        vb_in = sems("vb_in")
        xr_in, xr_made, xa_out = sems("xr_in"), sem("xr_made"), sems("xa_out")
        sm_made, max_made = sem("sm_made"), sem("max_made")
        ct_made, c_made, c_in = sem("ct_made"), sem("c_made"), sems("c_in")
        s_made, exp_made, sel_made = sem("s_made"), sem("exp_made"), sem("sel_made")
        y_made, y_copied, y_normal = sem("y_made"), sem("y_copied"), sem("y_normal")
        pj_made, xadd_made = sem("pj_made"), sem("xadd_made")
        cnt_made, tot_made = sem("cnt_made"), sem("tot_made")
        rt_dve, rt_pe = sem("rt_dve"), sem("rt_pe")
        pos_made, scattered, list_init, w1_in, w2_in = sem("pos_made"), sem("scattered"), sem("list_init"), sem("w1_in"), sem("w2_in")
        AHEAD = 6
        SLOTS = 8
        xs_in, tt_made, xT_made, h_made, hg_made, hh_made, hl_made, o_made, ob_made = (
            sems("xs_in", SLOTS), sem("tt_made"), sem("xT_made"), sem("h_made"), sem("hg_made"), sem("hh_made"),
            sem("hl_made"), sem("o_made"), sem("ob_made"))
        xg_in, ob_out = sems("xg_in", SLOTS), sems("ob_out", SLOTS)
        empt = sem("empt")

        rec_step, rec_made = sem("rec_step"), sem("rec_made")
        shift_step = sem("shift_step")
        consts = sem("consts")
        apart = sem("apart")

        block = ctx.enter_context(nc.Block())

        def after(eng, signal, value):
            if not isinstance(value, int) or value > 0:
                eng.wait_ge(signal, value)

        def wait_apart(eng, signal, value):
            eng.wait_ge(signal, value)
            eng.sem_inc(apart, 1)

        def pairs(eng, count, body, first=0):
            with eng.Fori(first, first + count) as i:
                for p in range(2):
                    body(i * 2 + p, i, p)

        def stage_a(eng, body):
            for n in (0, 1):
                body(n, 0, n)
            pairs(eng, B // 2 - 1, body, 1)

        def load_group(eng, n, p, g, which=(0, 1)):
            for r in range(len(Q_ROWS)):
                for w in which:
                    st, part, rows = ((qs, 1, Q_ROWS), (ks, 0, K_ROWS))[w]
                    eng.dma_start(st[r * D:(r + 1) * D, p, g, :, :],
                                  qk_d[part][rows[r], g * HG * D:(g + 1) * HG * D, bass.ds(n * S, S)]
                                  .rearrange("(h d) n -> d h n", d=D)).then_inc(grp_in[p][g], 16)

        @block.sync
        def _(sp):
            sp.dma_start(wk_f[:, :, 0:3 * E], w_kqv.rearrange("(k p) c -> p k c", p=P)).then_inc(cst_in, 16)
            sp.dma_start(wk_f[:, :, 3 * E:], wg.rearrange("(k p) c -> p k c", p=P)).then_inc(cst_in, 16)
            sp.dma_start(bqk[:, :], b_kqv[0:2 * E].rearrange("(c p) -> p c", p=P), allow_slow_non_contiguous=True).then_inc(cst_in, 16)
            sp.dma_start(bv[:, :, :].rearrange("p h d -> p (h d)"),
                         b_kqv[2 * E:3 * E].partition_broadcast(P)).then_inc(cst_in, 16)
            sp.dma_start(bp[:, :], b_proj.partition_broadcast(P)).then_inc(cst_in, 16)
            sp.dma_start(sl[R_ALIBI:R_ALIBI + 3, 0, :], slopes.partition_broadcast(3)).then_inc(cst_in, 16)
            sp.wait_ge(const_made, 11)
            for j in range(HG):
                sp.dma_start(wp[32 * j:32 * j + D, :, :],
                             w_proj.rearrange("(g j d) n -> j d g n", g=NG, d=D)[j]).then_inc(cst_in, 16)

            def store(n, p):
                sp.wait_ge(xw_made, n + 1)
                sp.dma_start(xnp[:, bass.ds(n * TB, TB), 0:2 * E], xw[p]).then_inc(xnp_in[p], 16)
                sp.wait_ge(we_lo, n + 1)
                for j in range(2):
                    sp.dma_start(ws_d[bass.ds(n, 1), :, j].rearrange("x p a w -> p (x a) w"),
                                 wsp[j].rearrange("p (a w) -> p a w", a=2)).then_inc(we_out, 16)
                for c in range(4):
                    sp.wait_ge(lo_made, 4 * n + c + 1)
                    for s in range(PARTS):
                        sp.dma_start(qk_d[c // 2][s, (c % 2) * P:(c % 2 + 1) * P, bass.ds(n * S, S)],
                                     pt[c][:, s, :]).then_inc(parts_out[c], 16)
                sp.wait_ge(v_used, 4 * n + 4)
                sp.dma_start(v_d[bass.ds(n, 1)].rearrange("b p c -> p (b c)"),
                             vt[:, p].rearrange("p t h w -> p (t h w)")).then_inc(v_out[p], 16)

            def a(n, i, p):
                after(sp, x_made, n - 1)
                sp.dma_start(xin[p], x_t[bass.ds(n, 1)].rearrange("b p t e -> p (b t) e")).then_inc(x_in[p], 16)
                after(sp, we_lo, n)
                sp.dma_start(wst[:, 0:1024].rearrange("p (k f) -> p k f", k=EC),
                             w1[bass.ds(n, 1)].rearrange("x (k p) f -> p (x k) f", p=P)).then_inc(we_in, 16)
                sp.dma_start(wst[:, 1024:2048].rearrange("p (k f) -> p k f", k=FC),
                             w2[bass.ds(n, 1)].rearrange("x (k p) f -> p (x k) f", p=P)).then_inc(we_in, 16)
                if not isinstance(n, int) or n > 0:
                    store(n - 1, 1 - p)

            stage_a(sp, a)
            store(B - 1, 1)

            def load_v(n, p):
                sp.dma_start(vt[:, p].rearrange("p t h w -> p (t h w)"),
                             v_d[bass.ds(n, 1)].rearrange("b p c -> p (b c)")).then_inc(vb_in[p], 16)

            def load_x(n, p):
                sp.dma_start(xr[:, p], x_t[bass.ds(n, 1)].rearrange("b p t e -> p (b t) e")).then_inc(xr_in[p], 16)

            for c in range(4):
                sp.wait_ge(parts_out[c], 16 * PARTS * B)
            for p in range(2):
                sp.wait_ge(v_out[p], 16 * B // 2)
            sp.wait_ge(we_out, 32 * B)
            for g in range(NG):
                load_group(sp, 0, 0, g, (0,))
            load_v(0, 0)
            sp.wait_ge(rows_made, 1)
            for st in (qs, ks):
                sp.dma_start(st[R_ALIBI:P, 1], st[R_ALIBI:P, 0]).then_inc(rows_in, 16)
            for g in range(NG):
                load_group(sp, 1, 1, g)
            load_x(0, 0)
            load_v(1, 1)
            load_x(1, 1)

            def b(n, i, p, more=True):
                for g in range(NG):
                    if more:
                        sp.wait_ge(s_made, NSJ * (NG * n + g + 1))
                        load_group(sp, n + 2, p, g)
                if more:
                    sp.wait_ge(y_made, NG * n + NG + 2)
                    load_v(n + 2, p)
                sp.wait_ge(xadd_made, 2 * n + 2 + 1)
                sp.dma_start(xa_t[bass.ds(n, 1)].rearrange("b p t e -> p (b t) e"), xr[:, p]).then_inc(xa_out[p], 16)
                if more:
                    sp.wait_ge(xa_out[p], 16 * (i + 1))
                    load_x(n + 2, p)

            pairs(sp, LOOPED // 2, b)
            b(B - 2, B // 2 - 1, 0, False)
            sp.wait_ge(scattered, 16 * NT)
            for a_ in range(2):
                sp.dma_start(w1_sb[:, :, a_, :], ws_d[:, :, a_, 0, :].rearrange("x p w -> p x w")).then_inc(w1_in, 16)
            sp.wait_ge(s_made, NSJ * NG * (B - 1))
            sp.dma_start(w2_h, ws_d[:, :, 0, 1, :].rearrange("x p w -> p x w")).then_inc(w2_in, 16)
            sp.dma_start(w2_l, ws_d[:, :, 1, 1, :].rearrange("x p w -> p x w")).then_inc(w2_in, 16)
            b(B - 1, B // 2 - 1, 1, False)

            def load_tile(s, k, q):
                sp.dma_start(xs_sb[:, q, :].bitcast(I32), xs_d[bass.ds(s * P, P), :]).then_inc(xs_in[q], 16)

            for q in range(SLOTS):
                load_tile(q, 0, q)
            with sp.Fori(1, TILES // SLOTS) as k:
                for q in range(SLOTS):
                    sp.wait_ge(ob_out[q], k * 16)
                    load_tile(k * SLOTS + q, k, q)
            for q in range(SLOTS):
                sp.wait_ge(ob_out[q], 16 * (TILES // SLOTS))

        @block.gpsimd
        def _(pool):
            step = [0]

            def mark(ins):
                step[0] += 1
                ins.then_inc(pool_step, 1)
                pool.wait_ge(pool_step, step[0])

            mark(pool.memset(epst[:, :], EPS))
            for m in (id16, idb, idf):
                pool.memset(m[:, :], 0.0).then_inc(pool_step, 1)
            pool.memset(ones[:, :], 1.0).then_inc(pool_step, 1)
            pool.memset(tri[:, :], 1.0).then_inc(pool_step, 1)
            pool.memset(maxmask[:, :], 0.0).then_inc(pool_step, 1)
            step[0] += 6
            mark(pool.memset(wp[:, :, :], 0.0))
            pool.sem_inc(const_made, 1)
            for m in (id16, idb, idf):
                pool.affine_select(out=m[:, :], in_=m[:, :], compare_op=ALU.not_equal, fill=1.0, base=0,
                                   pattern=[[-1, P]], channel_multiplier=1).then_inc(const_made, 1)
            pool.affine_select(out=tri[:, :], in_=tri[:, :], compare_op=ALU.is_ge, fill=0.0, base=-1,
                               pattern=[[1, P]], channel_multiplier=-1).then_inc(const_made, 1)
            pool.affine_select(out=maxmask[:, :], in_=maxmask[:, :], compare_op=ALU.is_ge, fill=NEG, base=0,
                               pattern=[[-1, P]], channel_multiplier=1).then_inc(const_made, 1)
            pool.memset(seg[:, :, :], 1.0).then_inc(const_made, 1)
            for p in range(2):
                pool.memset(vt[:, p].rearrange("p t h w -> p (t h) w")[:, :, D:VW], 1.0).then_inc(const_made, 1)
            pool.memset(empty[:, :], 0.0).then_inc(const_made, 1)
            pool.memset(thr[:, :], 0.0).then_inc(const_made, 1)
            base = 11
            def ints(pattern, n, b0, out_ap, chan=0):
                mark(pool.iota(iot[:, 0:n], pattern=pattern, base=b0, channel_multiplier=chan))
                mark(pool.tensor_copy(out_ap, iot[:, 0:n]))

            ints([[-1, X], [0, NT]], X * NT, X, rank8[:, :, :].rearrange("p a b -> p (a b)"))
            ints([[0, X], [P, NT]], X * NT, 0, lim[:, :, :].rearrange("p a b -> p (a b)"))
            ints([[1, TILES], [0, X]], TILES * X, 0, sno[:, :, :].rearrange("p a b -> p (a b)"))
            mark(pool.iota(tok[:, :], pattern=[[P, NT]], base=0, channel_multiplier=1))
            pool.wait_ge(const_made, base)
            mark(pool.memset(seg[:, :, 0:1], 0.0))
            mark(pool.memset(bits[:, :, :], 0))
            for k in range(BITS):
                pool.memset(bits[:, k, :], 1 << (BITS - 1 - k)).then_inc(pool_step, 1)
            step[0] += BITS
            mark(pool.memset(empty[:, 2 * E:2 * E + 2].bitcast(I32), NO_TOKEN))
            pool.sem_inc(consts, 1)

            rows = slice(R_ALIBI, P)
            b0 = (R_FAR - 1 - R_ALIBI) * FAR
            mark(pool.memset(k_rows[rows, :], 1.0))
            mark(pool.affine_select(out=k_rows[rows, :], in_=k_rows[rows, :], compare_op=ALU.is_ge, fill=0.0, base=b0,
                                    pattern=[[1, S]], channel_multiplier=-FAR))
            mark(pool.affine_select(out=k_rows[rows, :], in_=k_rows[rows, :], compare_op=ALU.is_ge, fill=0.0,
                                    base=FAR - 1 - b0, pattern=[[-1, S]], channel_multiplier=FAR))
            mark(pool.memset(k_rows[R_ALIBI:R_FAR, :], 1.0))
            mark(pool.iota(posi[R_ALIBI:R_SHIFT, :], pattern=[[1, S]], base=-MID, channel_multiplier=0))
            mark(pool.tensor_copy(k_rows[R_ALIBI:R_SHIFT, :], posi[R_ALIBI:R_SHIFT, :]))
            mark(pool.memset(q_rows[rows, :], 0.0))
            mark(pool.affine_select(out=q_rows[rows, :], in_=q_rows[rows, :], compare_op=ALU.is_ge, fill=NEG, base=b0,
                                    pattern=[[1, S]], channel_multiplier=-FAR))
            pool.sem_inc(consts, 1)
            pool.wait_ge(rows_in, 32)
            rows_base = step[0]

            def a(n, i, p):
                if p == 1:
                    after(pool, lo_made, 4 * n)
                    pool.tensor_copy(qs[R_ALIBI:R_SHIFT, 0, bass.ds(i, 1)].rearrange("p g h n -> p (g h) n"),
                                     sl[R_ALIBI:R_SHIFT, 6, bass.ds(i * HG, HG)][:, :, None].broadcast_to([3, HG, S])
                                     ).then_inc(pool_step, 1)
                    pool.wait_ge(pool_step, i + (rows_base + 1))
                for c in range(4):
                    pool.wait_ge(mid_made, 4 * n + c + 1)
                    pool.tensor_tensor(pt[c][:, 2, :], r1[c % 2], pt[c][:, 1, :], ALU.subtract).then_inc(lo_made, 1)

            stage_a(pool, a)
            step[0] += NG
            pool.sem_inc(rows_made, 1)

            def normalise(n, g):
                pool.wait_ge(rec_made, NG * n + g + 1)
                if g == 0:
                    pool.wait_ge(pj_made, 2 * n + 2)
                pool.tensor_tensor(yn[:, g, :], ysb[:, g % 2, :], rec_wide[:, g % 2, :], ALU.mult).then_inc(y_normal, 1)

            def b(n, i, p, extra=None):
                pool.wait_ge(xr_in[p], 16 * (i + 1))
                pool.tensor_tensor(xr[:, p], xr[:, p], bp[:, None, :].broadcast_to([P, TB, E]), ALU.add).then_inc(xr_made, 1)
                for g in range(NG):
                    for h in range(HG):
                        wait_apart(pool, exp_made, NSJ * (NG * n + g) + 3 * (h + 1) + 3)
                        v = pr_all[:, HG * (g % 2) + h, 0:W_R0].rearrange("p (t q) -> p t q", t=TB)
                        pool.affine_select(out=v, in_=v, compare_op=ALU.is_ge, fill=0.0, base=0,
                                           pattern=[[0, TB], [1, P]], channel_multiplier=-1).then_inc(sel_made, 1)
                        if extra:
                            for j in range(2):
                                extra(2 * (HG * g + h) + j)
                        if h == 1 and g >= 2:
                            normalise(n, g - 2)
                normalise(n, 2)
                normalise(n, 3)

            pool.wait_ge(exp_made, 3 + 1)
            pool.dma_start(xs_d.rearrange("(s p) c -> p s c", p=P),
                           empty[:, :].bitcast(I32)[:, None, :].broadcast_to([P, TILES, ROW // 2])).then_inc(list_init, 16)
            pairs(pool, LOOPED // 2, b)

            def scatter(t):
                pool.indirect_dma_start(out=xs_d, out_offset=bass.IndirectOffsetOnAxis(ap=pos[:, t:t + 1].bitcast(U32), axis=0),
                                        in_=xnp[:, t, :].bitcast(I32), in_offset=None).then_inc(scattered, 16)

            pool.wait_ge(pos_made, 1)
            pool.wait_ge(list_init, 16)
            for p in range(2):
                pool.wait_ge(xnp_in[p], 16 * B // 2)
            b(B - 2, B // 2 - 1, 0, scatter)
            b(B - 1, B // 2 - 1, 1)

            def tile_c(s, k, q):
                token = xs_sb[:, q, 2 * E:2 * E + 2].bitcast(U32)
                wait_apart(pool, xs_in[q], 16 * (k + 1))
                pool.indirect_dma_start(out=xg[:, q, :], out_offset=None, in_=xa_d,
                                        in_offset=bass.IndirectOffsetOnAxis(ap=token, axis=0),
                                        bounds_check=T - 1, oob_is_err=False).then_inc(xg_in[q], 16)

            def scatter_c(s, k, q):
                token = xs_sb[:, q, 2 * E:2 * E + 2].bitcast(U32)
                wait_apart(pool, ob_made, s + 1)
                pool.indirect_dma_start(out=out_rows, out_offset=bass.IndirectOffsetOnAxis(ap=token, axis=0),
                                        in_=ob[:, q, :], in_offset=None,
                                        bounds_check=T - 1, oob_is_err=False).then_inc(ob_out[q], 16)

            for p in range(2):
                pool.wait_ge(xa_out[p], 16 * B // 2)
            mark(pool.memset(xg[:, :, :], 0.0))
            for q in range(AHEAD):
                tile_c(q, 0, q)
            with pool.Fori(0, TILES // SLOTS - 1) as k:
                for q in range(SLOTS):
                    s2 = q + AHEAD
                    tile_c(k * SLOTS + s2, k + s2 // SLOTS, s2 % SLOTS)
                    scatter_c(k * SLOTS + q, k, q)
            k = TILES // SLOTS - 1
            for q in range(SLOTS):
                s2 = q + AHEAD
                if s2 < SLOTS:
                    tile_c(k * SLOTS + s2, k, s2)
                scatter_c(k * SLOTS + q, k, q)

        @block.scalar
        def _(act):
            act.sem_inc(exp_made, 3)
            act.sem_inc(y_copied, 1)
            act.wait_ge(cst_in, 160)
            act.activation(w_h[:, :, :], wk_f, ACT.Copy, scale=WS).then_inc(w_split, 1)
            act.activation(bqk[:, :], bqk[:, :], ACT.Copy, scale=WS).then_inc(act_step, 1)
            act.wait_ge(act_step, 1)
            act.wait_ge(w_split, 2)
            act.wait_ge(q8, 1)
            act.wait_ge(consts, 2)
            for st, one in ((ks, k_rows), (qs, q_rows)):
                act.dma_start(st[R_ALIBI:P, 0].rearrange("p g h n -> p (g h) n"),
                              one[R_ALIBI:P, None, :].broadcast_to([P - R_ALIBI, H, S])).then_inc(rows_in, 16)

            def a(n, i, p):
                act.wait_ge(stats, n + 1)
                act.activation(std[:, :], mv[:, :, 1], ACT.Sqrt, bias=epst[:, 0:1]).then_inc(std_made, 1)
                act.wait_ge(t_made, n + 1)
                after(act, v_made, 4 * n - 4)
                for a_ in range(2):
                    act.activation(xt[p][:, a_].rearrange("p k n -> p (k n)"), bank[a_].bitcast(F16),
                                   ACT.Copy).then_inc(t_used, 1)
                act.wait_ge(we_in, 32 * (n + 1))
                after(act, we_out, 32 * n)
                act.activation(wsp[0], wst, ACT.Copy, scale=WS).then_inc(we_hi, 1)
                def hi(c):
                    act.wait_ge(qk_made, 4 * n + c + 1)
                    after(act, parts_out[c], 16 * PARTS * n)
                    act.activation(pt[c][:, 0, :], bank[2 + c], ACT.Identity, bias=bqk[:, c:c + 1]).then_inc(hi_made, 1)

                def mid(c):
                    act.wait_ge(r1_made, 4 * n + c + 1)
                    act.activation(pt[c][:, 1, :], r1[c % 2], ACT.Copy).then_inc(mid_made, 1)

                hi(0)
                for c in range(4):
                    if c < 3:
                        hi(c + 1)
                    mid(c)

            stage_a(act, a)

            act.wait_ge(q8, 2)
            act.activation(pe8[:, :, :], lg[:, :, :], ACT.Exp).then_inc(exp8, 1)

            def shift_rows(n1, p1):
                act.wait_ge(c_made, n1 + 1)
                for r in range(2):
                    act.dma_start(qs[R_SHIFT + r:R_SHIFT + r + 1, p1].rearrange("p g h n -> p (g h) n"),
                                  cc[:, p1, r, :]).then_inc(c_in[p1], 16)

            def copy_y(n, g):
                act.wait_ge(y_made, NG * n + g + 1 + 2)
                act.wait_ge(y_normal, NG * n + g + 1)
                act.activation(ysb[:, g % 2, :], bank[5], ACT.Copy).then_inc(y_copied, 1)

            def b(n, i, p, more=True):
                for g in range(NG):
                    act.wait_ge(y_made, NG * n + g + 1)
                    for h in range(HG):
                        buf = pr_all[:, HG * (g % 2) + h, :]
                        for j, (c0, w) in enumerate(((W_R0, 384), (W_R1, 384), (W_DIAG, 512))):
                            act.wait_ge(s_made, NSJ * (NG * n + g) + 3 * h + j + 1)
                            act.activation(buf[:, c0:c0 + w], bank[2 + j][:, 0:w], ACT.Exp, scale=SCORE)\
                               .then_inc(exp_made, 1)
                            if g >= 1 and h == 3 and j == 1:
                                copy_y(n, g - 1)
                if more:
                    shift_rows(n + 1, 1 - p)
                copy_y(n, NG - 1)

            for c in range(4):
                act.wait_ge(parts_out[c], 16 * PARTS * B)
            for g in range(NG):
                load_group(act, 0, 0, g, (1,))
            act.wait_ge(rows_in, 64)
            shift_rows(0, 0)
            pairs(act, LOOPED // 2, b)
            b(B - 2, B // 2 - 1, 0)
            b(B - 1, B // 2 - 1, 1, False)

            def gelu(s, q):
                act.wait_ge(h_made, s + 1)
                after(act, hl_made, s - 1)
                act.activation(hg[:, q, :], bank[2 + q], ACT.Gelu, scale=1.0 / WS).then_inc(hg_made, 1)
                act.wait_ge(hg_made, s + 1)
                after(act, o_made, s - 1)
                act.activation(hh[:, q, 0, :], hg[:, q, :], ACT.Copy).then_inc(hh_made, 1)

            gelu(0, 0)
            gelu(1, 1)
            with act.Fori(1, TILES // 2) as k:
                for q in range(2):
                    gelu(2 * k + q, q)

        @block.vector
        def _(dve):
            step = [0]

            def mark(ins):
                step[0] += 1
                ins.then_inc(dve_step, 1)
                dve.wait_ge(dve_step, step[0])

            dve.sem_inc(y_normal, 2)
            dve.sem_inc(xadd_made, 1)
            dve.wait_ge(w_split, 1)
            mark(dve.scalar_tensor_tensor(out=w_l[:, :, :], in0=wk_f, scalar=WS, in1=w_h[:, :, :],
                                          op0=ALU.mult, op1=ALU.subtract))
            dve.sem_inc(w_split, 1)
            mark(dve.tensor_scalar(sl[R_ALIBI:R_SHIFT, 1, :], sl[R_ALIBI:R_SHIFT, 0, :], 1.0 / SCORE, None, ALU.mult))
            al = slice(R_ALIBI, R_SHIFT)
            dve.wait_ge(const_made, 4)
            for r in range(3):
                mark(dve.tensor_copy(slb[al, r, :], sl[al, 1 + r, :]))
                if r < 2:
                    mark(dve.tensor_tensor(sl[al, 2 + r, :], sl[al, 1 + r, :], slb[al, r, :], ALU.subtract))
            mark(dve.tensor_scalar(sl[al, 4, :], slb[al, 0, :], idf[al, R_ALIBI:R_ALIBI + 1], None, ALU.mult))
            for r in (1, 2):
                mark(dve.scalar_tensor_tensor(out=sl[al, 4 + r, :], in0=slb[al, r, :],
                                              scalar=idf[al, R_ALIBI + r:R_ALIBI + r + 1],
                                              in1=sl[al, 3 + r, :], op0=ALU.mult, op1=ALU.add))
            dve.sem_inc(q8, 1)
            mark0 = step[0]
            A_STEPS = 4

            def a(n, i, p):
                def link(ins, k):
                    ins.then_inc(dve_step, 1)
                    dve.wait_ge(dve_step, mark0 + n * A_STEPS + k)

                dve.wait_ge(x_in[p], 16 * (i + 1))
                for t in range(TB):
                    last = dve.bn_stats(bst[:, t, :], xin[p][:, t, :])
                last.then_inc(dve_step, 1)
                wait_apart(dve, dve_step, mark0 + n * A_STEPS + 1)
                for t in range(TB):
                    last = dve.bn_aggr(mv[:, t, :], bst[:, t, :])
                last.then_inc(stats, 1)
                dve.wait_ge(std_made, n + 1)
                link(dve.reciprocal(rstd[:, :], std[:, :]), 2)
                after(dve, xw_made, n)
                for t in range(TB):
                    last = dve.tensor_scalar(xn[:, t, :], xin[p][:, t, :], mv[:, t, 0:1], rstd[:, t:t + 1],
                                             ALU.subtract, ALU.mult)
                link(last, 3)
                dve.sem_inc(x_made, 1)
                after(dve, t_made, n - 1)
                after(dve, xnp_in[p], 16 * i)
                link(dve.tensor_copy(xw[p][:, :, 0:E], xn), 4)
                dve.tensor_tensor(xw[p][:, :, E:2 * E], xn, xw[p][:, :, 0:E], ALU.subtract).then_inc(xw_made, 1)
                dve.wait_ge(we_hi, n + 1)
                dve.scalar_tensor_tensor(out=wsp[1], in0=wst, scalar=WS, in1=wsp[0], op0=ALU.mult,
                                         op1=ALU.subtract).then_inc(we_lo, 1)
                for c in range(4):
                    dve.wait_ge(hi_made, 4 * n + c + 1)
                    after(dve, lo_made, 4 * n + c - 1)
                    dve.scalar_tensor_tensor(out=r1[c % 2], in0=bank[2 + c], scalar=bqk[:, c:c + 1],
                                             in1=pt[c][:, 0, :], op0=ALU.add, op1=ALU.subtract).then_inc(r1_made, 1)
                after(dve, v_out[p], 16 * i)
                for t in range(TB):
                    dve.wait_ge(v_made, 4 * n + t + 1)
                    vb = bank[6 + t % 2]
                    dve.scalar_tensor_tensor(out=vt[:, p, t, :, 0:D], in0=vb[:, 0:E].rearrange("p (h d) -> p h d", h=H),
                                             scalar=1.0 / WS, in1=bv[:, :, :], op0=ALU.mult, op1=ALU.add)
                    dve.tensor_scalar(lg[:, bass.ds(4 * n + t, 1), :].rearrange("p a b -> p (a b)"), vb[:, E:E + X],
                                      1.0 / WS, None, ALU.mult).then_inc(v_used, 1)

            stage_a(dve, a)
            step[0] += A_STEPS * B

            dve.wait_ge(v_used, NT)
            dve.wait_ge(consts, 1)
            bc = lambda ap: ap[:, :, None].broadcast_to([P, NT, X])
            mark(dve.tensor_reduce(r32[:, 0, :], lg[:, :, :], AX, ALU.max))
            mark(dve.tensor_tensor(lg[:, :, :], lg[:, :, :], bc(r32[:, 0, :]), ALU.subtract))
            dve.sem_inc(q8, 1)
            dve.memset(bank[5], 0.0).then_inc(y_copied, 1)
            dve.wait_ge(exp8, 1)
            mark(dve.tensor_reduce(r32[:, 1, :], pe8[:, :, :], AX, ALU.add))
            mark(dve.reciprocal(r32[:, 2, :], r32[:, 1, :]))
            mark(dve.tensor_tensor(pr[:, :, :].rearrange("p e t -> p t e"), pe8[:, :, :], bc(r32[:, 2, :]), ALU.mult))

            def row_max(n1, p1, g, k):
                u = NU * (NG * n1 + g) + k
                qt, hs = UNITS[k]
                w = (qt + 1) * P
                dve.wait_ge(sm_made, u + 1)
                src = bank[(NU * g + k) % 2][:, 0:w * len(hs)].rearrange("p (h c) -> p h c", c=w)
                h0 = g * HG + hs[0]
                dve.tensor_reduce(mx[:, p1, qt, h0:h0 + len(hs)], src, AX, ALU.max).then_inc(max_made, 1)

            def make_shift(n1, p1):
                dve.wait_ge(ct_made, n1 + 1)
                dve.tensor_scalar(cc[:, p1, 0, :], bank[7][0:H, :], -1.0, None, ALU.mult).then_inc(shift_step, 1)
                dve.wait_ge(shift_step, n1 + 1)
                dve.scalar_tensor_tensor(out=cc[:, p1, 1, :], in0=bank[7][0:H, :], scalar=-1.0, in1=cc[:, p1, 0, :],
                                         op0=ALU.mult, op1=ALU.subtract).then_inc(c_made, 1)

            def invert(n, g):
                k0 = 2 * (NG * n + g)
                dve.wait_ge(y_copied, NG * n + g + 3)
                dve.transpose(yt[:, :, :].rearrange("p b c -> p (b c)"), ysb[:, g % 2, :]).then_inc(rec_step, 1)
                dve.wait_ge(rec_step, k0 + 1)
                dve.reciprocal(rec[:, :], yt[:, :, D]).then_inc(rec_step, 1)
                dve.wait_ge(rec_step, k0 + 2)
                dve.wait_ge(y_normal, NG * n + g + 1)
                dve.transpose(rec_wide[:, g % 2, :], rec[:, :, None].broadcast_to([P, S // 32, 32])
                              ).then_inc(rec_made, 1)

            def residual(n, p, j):
                if j == 0:
                    dve.wait_ge(xr_made, n + 1)
                dve.wait_ge(pj_made, 2 * n + j + 1 + 2)
                v = xr[:, p, 2 * j:2 * j + 2, :]
                dve.tensor_tensor(v, bank[7 - j].rearrange("p (t e) -> p t e", t=2), v, ALU.add).then_inc(xadd_made, 1)

            bisect_base = step[0]

            def bisect_count(it):
                k0 = bisect_base + 4 * it
                dve.tensor_tensor(cand[:, :].bitcast(U32), thr[:, :].bitcast(U32),
                                  bits[:, bass.ds(it, 1), :].rearrange("p a e -> p (a e)"),
                                  ALU.bitwise_or).then_inc(dve_step, 1)
                dve.wait_ge(dve_step, k0 + 1)
                dve.tensor_tensor(hit[:, :, :], pr[:, :, :], cand[:, :, None].broadcast_to([P, X, NT]),
                                  ALU.is_ge).then_inc(dve_step, 1)
                dve.wait_ge(dve_step, k0 + 2)
                with nc.allow_low_precision("counts up to 32 are exact"):
                    dve.tensor_reduce(cnt[:, :], hit[:, :, :], AX, ALU.add).then_inc(cnt_made, 1)

            def bisect_take(it):
                k0 = bisect_base + 4 * it
                dve.wait_ge(tot_made, it + 1)
                dve.tensor_scalar(acc[:, :], bank[7][:, 0:X], float(CAP), None, ALU.is_ge).then_inc(dve_step, 1)
                wait_apart(dve, dve_step, k0 + 3)
                dve.copy_predicated(thr[:, :], acc[:, :], cand[:, :]).then_inc(dve_step, 1)
                dve.wait_ge(dve_step, k0 + 4)

            for g in range(NG):
                for k in range(NU):
                    row_max(0, 0, g, k)
            make_shift(0, 0)

            def b(n, i, p, more=True, bis=True):
                for g in range(NG):
                    it = n * BPB + sum(BIS[:g])
                    if bis:
                        bisect_count(it)
                    for k in range(NSJ):
                        u = NSJ * g + k
                        if more and u < NU * NG:
                            row_max(n + 1, 1 - p, u // NU, u % NU)
                        if more and u == TURN:
                            make_shift(n + 1, 1 - p)
                        if k == 3 and g >= 2:
                            invert(n, g - 2)
                        if bis and k == 4:
                            bisect_take(it)
                            if BIS[g] == 2:
                                bisect_count(it + 1)
                        if bis and k == 9 and BIS[g] == 2:
                            bisect_take(it + 1)
                for g in (2, 3):
                    invert(n, g)
                for j in range(2):
                    residual(n, p, j)

            pairs(dve, LOOPED // 2, b)
            step[0] += 4 * BPB * LOOPED

            e8 = lambda ap: ap[:, :, None].broadcast_to([P, X, NT])
            t32 = lambda ap: ap[:, None, :].broadcast_to([P, X, NT])
            by_t = lambda ap: ap[:, :, :].rearrange("p e t -> p t e")
            TT = lambda *a, **k: mark(dve.tensor_tensor(*a, **k))

            def offsets(dst, k):
                dve.wait_ge(rt_pe, k)
                mark(dve.tensor_copy(rr[2][:, :, :], bank[6][:, 256:512].rearrange("p (e t) -> p e t", e=X)))
                fl = lambda a_: a_[:, :, :].rearrange("p e t -> p (e t)")
                mark(dve.tensor_tensor_scan(fl(dst), fl(seg), fl(rr[2]), 0.0, ALU.mult, ALU.add))
                mark(dve.tensor_copy(r8[:, 2, :], dst[:, :, NT - 1]))
                TT(dst[:, :, :], dst[:, :, :], rr[2][:, :, :], ALU.subtract)
                TT(dst[:, :, :], bank[6][:, 0:256].rearrange("p (e t) -> p e t", e=X), dst[:, :, :], ALU.add)

            TT(gtb[:, :, :], pr[:, :, :], e8(thr), ALU.is_gt)
            with nc.allow_low_precision("counts up to 32 are exact"):
                mark(dve.tensor_reduce(cnt[:, :], gtb[:, :, :], AX, ALU.add))
            TT(hit[:, :, :], pr[:, :, :], e8(thr), ALU.is_equal)
            dve.sem_inc(rt_dve, 1)
            offsets(rr[0], 1)
            mark(dve.tensor_scalar(r8[:, 0, :], bank[7][:, 0:X], -1.0, float(CAP), ALU.mult, ALU.add))
            TT(rr[0][:, :, :], rr[0][:, :, :], e8(r8[:, 0, :]), ALU.is_lt)
            TT(rr[0][:, :, :], rr[0][:, :, :], hit[:, :, :], ALU.mult)
            TT(rr[0][:, :, :], rr[0][:, :, :], gtb[:, :, :], ALU.max)
            mark(dve.tensor_reduce(r32[:, 0, :], by_t(rr[0]), AX, ALU.max))
            TT(rr[0][:, :, :], rr[0][:, :, :], t32(r32[:, 0, :]), ALU.is_ge)
            TT(rr[1][:, :, :], rr[0][:, :, :], pr[:, :, :], ALU.mult)
            mark(dve.scalar_tensor_tensor(out=rr[1][:, :, :], in0=rr[0][:, :, :], scalar=-1.0, in1=rr[1][:, :, :],
                                          op0=ALU.add, op1=ALU.add))
            mark(dve.tensor_reduce(r32[:, 1, :], by_t(rr[1]), AX, ALU.max))
            TT(rr[1][:, :, :], rr[1][:, :, :], t32(r32[:, 1, :]), ALU.is_equal)
            TT(rr[1][:, :, :], rr[1][:, :, :], rank8[:, :, :], ALU.mult)
            mark(dve.tensor_reduce(r32[:, 2, :], by_t(rr[1]), AX, ALU.max))
            TT(hit[:, :, :], rr[1][:, :, :], t32(r32[:, 2, :]), ALU.is_equal)
            dve.sem_inc(rt_dve, 1)
            TT(rr[1][:, :, :], hit[:, :, :], pr[:, :, :], ALU.mult)
            mark(dve.tensor_reduce(r32[:, 3, :], by_t(rr[1]), AX, ALU.max))
            mark(dve.tensor_scalar(r32[:, 3, :], r32[:, 3, :], 1.0 / WS, None, ALU.mult))
            offsets(rr[0], 2)
            TT(rr[1][:, :, :], e8(r8[:, 2, :]), lim[:, :, :], ALU.is_gt)
            mark(dve.tensor_reduce(r8[:, 3, :], rr[1][:, :, :], AX, ALU.add))
            mark(dve.memset(r8[:, 0, :], 1.0))
            mark(dve.tensor_tensor_scan(r8[:, 4, :], r8[:, 0, :], r8[:, 3, :], 0.0, ALU.mult, ALU.add))
            TT(r8[:, 5, :], r8[:, 4, :], r8[:, 3, :], ALU.subtract)
            mark(dve.tensor_scalar(r8[:, 5, :], r8[:, 5, :], float(P), None, ALU.mult))
            TT(rr[0][:, :, :], rr[0][:, :, :], e8(r8[:, 5, :]), ALU.add)
            TT(rr[0][:, :, :], rr[0][:, :, :], hit[:, :, :], ALU.mult)
            mark(dve.tensor_reduce(r32[:, 4, :], by_t(rr[0]), AX, ALU.add))
            mark(dve.tensor_copy(pos[:, :], r32[:, 4, :]))
            for p in range(2):
                dve.wait_ge(xnp_in[p], 16 * B // 2)
            mark(dve.tensor_copy(xnp[:, :, 2 * E:2 * E + 2].bitcast(I32).rearrange("p t a -> p (t a)"), tok[:, :]))
            mark(dve.tensor_copy(xnp[:, :, 2 * E + 2:].bitcast(F32).rearrange("p t a -> p (t a)"), r32[:, 3, :]))
            dve.sem_inc(pos_made, 1)
            TT(ecmp[:, :, :], r8[:, 4, :][:, None, :].broadcast_to([P, TILES, X]), sno[:, :, :], ALU.is_le)
            mark(dve.tensor_reduce(eidf[:, :], ecmp[:, :, :], AX, ALU.add))
            mark(dve.tensor_scalar(eid[:, :], eidf[:, :], float(X - 1), None, ALU.min))
            dve.sem_inc(pos_made, 1)

            b(B - 2, B // 2 - 1, 0, True, False)
            b(B - 1, B // 2 - 1, 1, False, False)

            def take_x(s, q):
                dve.wait_ge(tt_made, s + 1)
                dve.tensor_copy(xT[:, q].rearrange("p a n -> p (a n)"), bank[q].bitcast(F16)[:, 0:512]).then_inc(xT_made, 1)

            def low(s, q):
                dve.wait_ge(hh_made, s + 1)
                dve.tensor_tensor(hh[:, q, 1, :], hg[:, q, :], hh[:, q, 0, :], ALU.subtract).then_inc(hl_made, 1)

            def combine(s, k, q):
                dve.wait_ge(o_made, s + 1)
                dve.wait_ge(xg_in[q], k * 16 + 16)
                after(dve, ob_out[q], k * 16)
                dve.scalar_tensor_tensor(out=ob[:, q, :], in0=bank[4 + q % 2][:, 0:E],
                                         scalar=xs_sb[:, q, 2 * E + 2:].bitcast(F32), in1=xg[:, q, :],
                                         op0=ALU.mult, op1=ALU.add).then_inc(ob_made, 1)

            def steps(s, k, tiles, more=SLOTS):
                for q in range(tiles):
                    combine(s + q, k, q)
                    if q < more:
                        take_x(s + q + 2, q % 2)
                    if q < more + 1:
                        low(s + q + 1, (q + 1) % 2)

            take_x(0, 0)
            take_x(1, 1)
            low(0, 0)
            steps(0, 0, SLOTS)
            with dve.Fori(1, TILES // SLOTS - 1) as k:
                steps(k * SLOTS, k, SLOTS)
            steps(TILES - SLOTS, TILES // SLOTS - 1, SLOTS, SLOTS - 2)

        @block.tensor
        def _(pe):
            pe.sem_inc(y_made, 2)
            pe.sem_inc(pj_made, 2)
            pe.wait_ge(const_made, 11)
            pe.wait_ge(w_split, 2)

            def six(out, lhs, rhs):
                terms = [(0, 0), (0, 1), (1, 0)]
                for k in range(EC):
                    for j, (a_, b_) in enumerate(terms):
                        last = pe.matmul(out, lhs(a_, k), rhs(b_, k), start=(k == 0 and j == 0),
                                         stop=(k == EC - 1 and j == 2))
                return last

            def a(n, i, p):
                pe.wait_ge(xw_made, n + 1)
                after(pe, t_used, 2 * n)
                for t in range(TB):
                    for a_ in range(2):
                        for k in range(EC):
                            last = pe.transpose(bank[a_].bitcast(F16)[:, k * S + t * P:k * S + (t + 1) * P],
                                                xw[p][:, t, (a_ * EC + k) * P:(a_ * EC + k + 1) * P], id16[:, :])
                last.then_inc(t_made, 1)
                pe.wait_ge(t_used, 2 * n + 2)
                W = (w_h, w_l)
                for c in range(4):
                    after(pe, r1_made, 4 * n + c - 3)
                    six(bank[2 + c], lambda a_, k: W[a_][:, k, c * P:(c + 1) * P],
                        lambda b_, k: xt[p][:, b_, k, :]).then_inc(qk_made, 1)
                for t in range(TB):
                    after(pe, v_used, 4 * n + t - 1)
                    last = six(bank[6 + t % 2][:, 0:E + X], lambda a_, k: xt[p][:, a_, k, t * P:(t + 1) * P],
                               lambda b_, k: W[b_][:, k, 2 * E:3 * E + X])
                    last.then_inc(v_made, 1)

            stage_a(pe, a)
            pe.wait_ge(r1_made, 4 * B)
            pe.wait_ge(v_used, 4 * B)
            pe.wait_ge(y_copied, 2)

            def max_unit(n1, p1, i1, g, k):
                u = NU * (NG * n1 + g) + k
                if k == 0:
                    pe.wait_ge(grp_in[p1][g], 16 * 12 * (i1 + 1))
                if not isinstance(n1, int) or u >= 2:
                    pe.wait_ge(max_made, u - 1)
                qt, hs = UNITS[k]
                w = (qt + 1) * P
                dst = bank[(NU * g + k) % 2]
                for j, h in enumerate(hs):
                    pe.matmul(dst[:, j * w:(j + 1) * w], qs[0:R_SHIFT, p1, g, h, qt * P:w],
                              ks[0:R_SHIFT, p1, g, h, 0:w], start=True, stop=False)
                    last = pe.matmul(dst[:, (j + 1) * w - P:(j + 1) * w], idb[:, :], maxmask[:, :],
                                     start=False, stop=True)
                last.then_inc(sm_made, 1)

            def scores(n, p, i, g, h, j):
                v = NSJ * (NG * n + g) + 3 * h + j
                if g == 0 and h == 0 and j == 0:
                    pe.wait_ge(c_in[p], 32 * (i + 1))
                pe.wait_ge(exp_made, v + 1)
                blocks = ([(0, P, 384, 0)], [(1, 2 * P, 256, 0), (2, 3 * P, P, 256)],
                          [(t, t * P, P, t * P) for t in range(TB)])[j]
                for t, q0, w, c0 in blocks:
                    last = pe.matmul(bank[2 + j][:, c0:c0 + w], ks[:, p, g, h, t * P:(t + 1) * P],
                                     qs[:, p, g, h, q0:q0 + w], start=True, stop=True)
                last.then_inc(s_made, 1)

            def with_v(n, p, i, g, k):
                if k == 0:
                    pe.wait_ge(sel_made, HG * (NG * n + g + 1))
                    pe.wait_ge(exp_made, NSJ * (NG * n + g + 1) + 3)
                    pe.wait_ge(y_copied, NG * n + g + 2)
                    if g == 0:
                        pe.wait_ge(vb_in[p], 16 * (i + 1))
                t, c0, q0, w = PIECES[k]
                for h in range(HG):
                    last = pe.matmul(bank[5][32 * h:32 * h + VW, q0:q0 + w], vt[:, p, t, g * HG + h, :],
                                     pr_all[:, HG * (g % 2) + h, c0:c0 + w], start=(k == 0),
                                     stop=(k == len(PIECES) - 1), skip_group_check=True)
                if k == len(PIECES) - 1:
                    last.then_inc(y_made, 1)

            def turn_max(n1, p1):
                pe.wait_ge(max_made, NU * NG * (n1 + 1))
                for t in range(TB):
                    last = pe.transpose(bank[7][0:H, t * P:(t + 1) * P], mx[:, p1, t, :], idf[:, :])
                last.then_inc(ct_made, 1)

            def project(n, groups):
                pe.wait_ge(y_normal, NG * n + groups[-1] + 1 + 2)
                pe.wait_ge(xadd_made, 2 * n + 1)
                for j in range(2):
                    for t in range(2):
                        for g in groups:
                            last = pe.matmul(bank[7 - j][:, t * E:(t + 1) * E],
                                             yn[:, g, (2 * j + t) * P:(2 * j + t + 1) * P], wp[:, g, :],
                                             start=(g == 0 and t == 0), stop=(g == NG - 1),
                                             skip_group_check=True)
                    if groups[-1] == NG - 1:
                        last.then_inc(pj_made, 1)

            def total(it):
                pe.wait_ge(cnt_made, it + 1)
                pe.matmul(bank[7][:, 0:X], ones[:, :], cnt[:, :], start=True, stop=True).then_inc(tot_made, 1)

            pe.wait_ge(rows_made, 1)
            for g in range(NG):
                for k in range(NU):
                    max_unit(0, 0, 0, g, k)
            turn_max(0, 0)
            pe.wait_ge(c_made, 1)
            pe.wait_ge(rows_in, 64)

            def b(n, i, p, more=True, bis=True):
                for g in range(NG):
                    it = n * BPB + sum(BIS[:g])
                    for k in range(NSJ):
                        u = NSJ * g + k
                        if more and u < NU * NG:
                            max_unit(n + 1, 1 - p, i + p, u // NU, u % NU)
                        if more and u == TURN:
                            pe.wait_ge(xadd_made, 2 * n + 1)
                            turn_max(n + 1, 1 - p)
                        scores(n, p, i, g, k // 3, k % 3)
                        if bis and k == 3:
                            total(it)
                        if bis and k == 8 and BIS[g] == 2:
                            total(it + 1)
                        if g >= 1 and 4 <= k <= 10:
                            with_v(n, p, i, g - 1, k - 4)
                for k in range(len(PIECES)):
                    with_v(n, p, i, 3, k)
                if more:
                    pe.wait_ge(c_made, n + 2)
                project(n, (0, 1, 2))
                project(n, (3,))

            pairs(pe, LOOPED // 2, b)

            def count_marks(k):
                pe.wait_ge(rt_dve, k)
                v = hit[:, :, :].rearrange("p e t -> p (e t)")
                pe.matmul(bank[6][:, 0:256], tri[:, :], v, start=True, stop=True)
                last = pe.matmul(bank[6][:, 256:512], ones[:, :], v, start=True, stop=True)
                if k == 1:
                    last = pe.matmul(bank[7][:, 0:X], ones[:, :], cnt[:, :], start=True, stop=True)
                last.then_inc(rt_pe, 1)

            pe.wait_ge(y_normal, NG * LOOPED + 2)
            pe.wait_ge(xadd_made, 2 * LOOPED + 1)
            count_marks(1)
            count_marks(2)
            pe.wait_ge(pos_made, 1)
            b(B - 2, B // 2 - 1, 0, True, False)
            b(B - 1, B // 2 - 1, 1, False, False)

            def turn_x(s, k, q):
                pe.wait_ge(xs_in[q], k * 16 + 16)
                for j in range(4):
                    last = pe.transpose(bank[q % 2].bitcast(F16)[:, j * P:(j + 1) * P], xs_sb[:, q, j * P:(j + 1) * P], id16[:, :])
                last.then_inc(tt_made, 1)

            def expert_of(s):
                return pe.value_load(eid[0:1, bass.ds(s, 1)], min_val=0, max_val=X - 1)

            def up(s, q, e):
                pe.wait_ge(xT_made, s + 1)
                after(pe, hg_made, s - 1)
                terms = [(0, 0), (0, 1), (1, 0)]
                for f in range(FC):
                    for k in range(EC):
                        for j, (a_, b_) in enumerate(terms):
                            c0 = k * FF + f * P
                            last = pe.matmul(bank[2 + q][:, f * P:(f + 1) * P],
                                             w1_sb[:, bass.ds(e, 1), a_, c0:c0 + P].rearrange("p x w -> p (x w)"),
                                             xT[:, q, b_ * EC + k, :], start=(k == 0 and j == 0),
                                             stop=(k == EC - 1 and j == 2))
                last.then_inc(h_made, 1)

            def down(s, q, e):
                pe.wait_ge(hl_made, s + 1)
                after(pe, ob_made, s - 1)
                w2p = (w2_h, w2_l)
                for f in range(FC):
                    for j, (a_, b_) in enumerate([(0, 0), (0, 1), (1, 0)]):
                        last = pe.matmul(bank[4 + q][:, 0:E], hh[:, q, a_, f * P:(f + 1) * P],
                                         w2p[b_][:, bass.ds(e, 1), f * E:(f + 1) * E].rearrange("p x w -> p (x w)"),
                                         start=(f == 0 and j == 0), stop=(f == FC - 1 and j == 2))
                last.then_inc(o_made, 1)

            pe.wait_ge(w1_in, 32)
            pe.wait_ge(w2_in, 32)
            pe.wait_ge(pos_made, 2)
            turn_x(0, 0, 0)
            up(0, 0, expert_of(0))
            turn_x(1, 0, 1)
            up(1, 1, expert_of(1))

            def steps(s, k, more=SLOTS):
                experts = [expert_of(s), expert_of(s + 1)]
                for q in range(SLOTS):
                    if q < more:
                        experts.append(expert_of(s + q + 2))
                    down(s + q, q % 2, experts[q])
                    if q < more:
                        turn_x(s + q + 2, k + (q + 2) // SLOTS, (q + 2) % SLOTS)
                        up(s + q + 2, q % 2, experts[q + 2])

            steps(0, 0)
            with pe.Fori(1, TILES // SLOTS - 1) as k:
                steps(k * SLOTS, k)
            steps(TILES - SLOTS, TILES // SLOTS - 1, SLOTS - 2)


_INS = ['L0_attn_x', 'L0_attn_W_kqv', 'L0_attn_b_kqv', 'L0_attn_W_proj', 'L0_attn_b_proj', 'L0_attn_slopes',
        'L0_ffn_Wg', 'L0_ffn_W1', 'L0_ffn_W2']


def kernel(**inputs):
    import numpy as _np
    import concourse.bacc as _bacc
    from concourse import mybir as _mybir
    from concourse.bass_utils import run_bass_kernel_spmd as _run

    nc = _bacc.Bacc("TRN2", target_bir_lowering=False, num_devices=1)
    arrays, args = {}, []
    for name in _INS:
        a = _np.ascontiguousarray(inputs[name])
        arrays[f"in_{name}_dram"] = a
        args.append(nc.dram_tensor(f"in_{name}_dram", a.shape, _mybir.dt.from_np(a.dtype), kind="ExternalInput").ap())
    args.append(nc.dram_tensor("out_0_dram", (B, S, E), _mybir.dt.float32, kind="ExternalOutput").ap())
    layer(nc, *args)
    r = _run(nc, [arrays], core_ids=[0])
    return r.results[0]["out_0_dram"]
```

```python
from contextlib import ExitStack

import concourse.bass as bass
from concourse import mybir

F32, F16, BF16 = mybir.dt.float32, mybir.dt.float16, mybir.dt.bfloat16
I32, U32 = mybir.dt.int32, mybir.dt.uint32
ALU = mybir.AluOpType
ACT = mybir.ActivationFunctionType
AX = mybir.AxisListType.X

P = 128
B, S, E, H, D = 8, 512, 256, 16, 16
T = B * S
NT = T // P
TB = S // P
EC = E // P
X, FF = 8, 512
FC = FF // P
CAP = T // X
SLOTS = 8
AHEAD = 6
TILES = NT + X
HG = 4
NG = H // HG
WS = 256.0
SCORE = 1.0 / (4.0 * WS * WS)
NEG = -1e30 / SCORE
EPS = 1e-5
PARTS = 3
Q_RUNS = ((0, 3, 0, 0), (3, 2, 1, 0), (5, 1, 2, 0))
K_RUNS = ((0, 3, 0, 1), (3, 2, 0, 1), (5, 1, 0, 0))
RUNS = len(Q_RUNS) + len(K_RUNS)
R_ALIBI = 6 * D
R_SHIFT = R_ALIBI + 3
R_FAR = R_SHIFT + 2
FAR = -(-S // (P - R_FAR + 1))
MID = 256
VW = D + 1
ROW = 2 * E + 4
BITS = 30
BIS = (2, 1, 2, 1)
BPB = sum(BIS)
COUNT_AT = (3, 3, 3, 1)
ROUTED = 5
NO_TOKEN = 1 << 20
UNITS = [(3, (h,)) for h in range(4)] + [(2, (h,)) for h in range(4)] + \
        [(1, (0, 1)), (1, (2, 3)), (0, (0, 1, 2, 3))]
NU = len(UNITS)
NSJ = 3 * HG
UNITS_AT = lambda u: range(u * 11 // 10, min((u + 1) * 11 // 10, NU * NG))
TURN = NU * NG * 10 // 11 + 1
PROJECT = {(1, 8): (0, 0), (1, 10): (0, 1), (2, 3): (1, 0), (2, 5): (1, 1)}
W_DIAG, W_R0, W_R1, W_R2 = 0, 512, 896, 1152
W_ALL = 1280
PIECES = [(0, W_R0, 128, 384), (0, 0, 0, 128), (1, W_R1, 256, 256), (2, W_R2, 384, 128),
          (1, 128, 128, 128), (2, 256, 256, 128), (3, 384, 384, 128)]


def layer(nc, x, w_kqv, b_kqv, w_proj, b_proj, slopes, wg, w1, w2, out):
    x_t = x.rearrange("b (t p) e -> b p t e", p=P)
    qk_d = [nc.dram_tensor(f"{n}_parts", [B, PARTS, D, H * S], BF16, kind="Internal").ap() for n in "kq"]
    v_d = nc.dram_tensor("v_rows", [B, P, TB * H * VW], F32, kind="Internal").ap()
    xa_d = nc.dram_tensor("x_plus_attention", [T, E], F32, kind="Internal").ap()
    ws_d = nc.dram_tensor("expert_parts", [X, P, 2, 2, 1024], F16, kind="Internal").ap()
    xs_d = nc.dram_tensor("sorted_rows", [TILES * P, ROW // 2], I32, kind="Internal").ap()
    out_rows = out.rearrange("b s e -> (b s) e")
    xa_t = xa_d.rearrange("(b t p) e -> b p t e", p=P, t=TB)

    with ExitStack() as ctx:
        def sb(name, shape, dt):
            return ctx.enter_context(nc.sbuf_tensor(name, shape, dt))

        def sem(name):
            return ctx.enter_context(nc.semaphore(name))

        def sems(name, n=2):
            return [sem(f"{name}{i}") for i in range(n)]

        ps = ctx.enter_context(nc.psum_tensor("ps", [P, 8, 512], F32))
        bank = [ps[:, i, :] for i in range(8)]

        id16 = sb("id16", [P, P], F16)
        idb = sb("idb", [P, P], BF16)
        idf = sb("idf", [P, P], F32)
        ones = sb("ones", [P, P], BF16)
        tri = sb("tri", [P, P], BF16)
        maxmask = sb("maxmask", [P, P], BF16)
        bits = sb("bits", [P, BITS, X], U32)
        epst = sb("epst", [P, 1], F32)
        seg = sb("seg", [P, X, NT], F32)
        rank8 = sb("rank8", [P, X, NT], F32)
        lim = sb("lim", [P, X, NT], F32)
        sno = sb("sno", [P, TILES, X], F32)
        iot = sb("iot", [P, TILES * X], I32)
        tok = sb("tok", [P, NT], I32)
        w_h = sb("w_h", [P, EC, 3 * E + X], F16)
        w_l = sb("w_l", [P, EC, 3 * E + X], F16)
        bqk = sb("bqk", [P, 4], F32)
        bv = sb("bv", [P, H, D], F32)
        bp = sb("bp", [P, E], F32)
        wp = sb("wp", [P, NG, E], F32)
        sl = sb("sl", [P, 7, H], F32)
        slb = sb("slb", [P, 3, H], BF16)
        qs = sb("qs", [P, 2, NG, HG, S], BF16)
        ks = sb("ks", [P, 2, NG, HG, S], BF16)
        pr_all = sb("pr_all", [P, 8, W_ALL], F32)
        vt = sb("vt", [P, 2, TB, H, VW], F32)
        xnp = sb("xnp", [P, NT, ROW], F16)
        ysb = sb("ysb", [P, 2, S], F32)
        yt = sb("yt", [P, S // 32, 32], F32)
        rec = sb("rec", [P, S // 32], F32)
        rec_wide = sb("rec_wide", [P, 2, S], F32)
        yn = sb("yn", [P, NG, S], F32)
        xr = sb("xr", [P, 2, TB, E], F32)
        mx = sb("mx", [P, 2, TB, H], F32)
        cc = sb("cc", [H, 2, S], BF16)
        w_low = sb("w_low", [P, 2, 512], F16)
        lg = sb("lg", [P, NT, X], F32)
        pe8 = sb("pe8", [P, NT, X], F32)
        pr = sb("pr", [P, X, NT], F32)
        thr = sb("thr", [P, X], F32)
        cand = sb("cand", [P, X], F32)
        hit = sb("hit", [P, X, NT], BF16)
        cnt = sb("cnt", [P, X], BF16)
        acc = sb("acc", [P, X], U32)
        r32 = sb("r32", [P, 6, NT], F32)
        r8 = sb("r8", [P, 6, X], F32)
        rr = [sb(f"rr{i}", [P, X, NT], F32) for i in range(3)]
        gtb = sb("gtb", [P, X, NT], BF16)
        pos = sb("pos", [P, NT], I32)
        ecmp = sb("ecmp", [P, TILES, X], F32)
        eidf = sb("eidf", [P, TILES], F32)
        place = sb("place", [P, SLOTS], F32)
        codes = sb("codes", [P, TILES // SLOTS], I32)

        posi = rec_wide[:, 0, :].bitcast(I32)
        k_rows = ysb[:, 0, :].bitcast(BF16)[:, 0:S]
        q_rows = ysb[:, 1, :].bitcast(BF16)[:, 0:S]

        flat = pr_all[:, :, :].rearrange("p a b -> p (a b)")
        at = [0]

        def cut(n_bytes, dt, pattern=None, **dims):
            n = n_bytes // 4
            v = flat[:, at[0]:at[0] + n]
            at[0] += n
            assert at[0] <= 8 * W_ALL
            v = v if dt == F32 else v.bitcast(dt)
            return v.rearrange(pattern, **dims) if pattern else v

        xin = [cut(4096, F32, "p (t e) -> p t e", t=TB) for _ in range(2)]
        old = [w[:, :, :].rearrange("p k c -> p (k c)") for w in (w_h, w_l)]
        wq = [w[:, 0:1024].bitcast(F32) for w in old]
        wq_part = [(w[:, 1024:1536], w_low[:, j, :]) for j, w in enumerate(old)]
        xn = cut(4096, F32, "p (t e) -> p t e", t=TB)
        xt = [cut(4096, F16, "p (a k n) -> p a k n", a=2, k=EC) for _ in range(2)]
        r1 = [cut(2048, F32) for _ in range(2)]
        bst = sb("bst", [P, TB, 6], F32)
        mv = sb("mv", [P, TB, 2], F32)
        std = sb("std", [P, TB], F32)
        rstd = sb("rstd", [P, TB], F32)
        pt = [ks[:, 1, c, 0:PARTS, :] for c in range(4)]
        wk_f = qs[:, 0, 0:2, :, :].rearrange("p a b c -> p (a b c)").bitcast(F32)[:, 0:EC * (3 * E + X)] \
            .rearrange("p (k c) -> p k c", k=EC)

        w1_sb = xnp[:, :, :].rearrange("p a b -> p (a b)")[:, 0:X * 2 * 1024] \
            .rearrange("p (x a w) -> p x a w", x=X, a=2)
        w2_h = qs[:, 0, :, :, :].rearrange("p a b c -> p (a b c)").bitcast(F16) \
            .rearrange("p (x w) -> p x w", x=X)
        w2_l = ks[:, 0, :, :, :].rearrange("p a b c -> p (a b c)").bitcast(F16) \
            .rearrange("p (x w) -> p x w", x=X)
        at[0] = 0
        xs_sb = cut(8 * ROW * 2, F16, "p (q c) -> p q c", q=8)
        xT = cut(2 * 4 * P * 2, F16, "p (q a c) -> p q a c", q=2, a=4)
        hg = cut(2 * FF * 4, F32, "p (q c) -> p q c", q=2)
        hh = cut(2 * 2 * FF * 2, F16, "p (q a c) -> p q a c", q=2, a=2)
        xg = cut(8 * E * 4, F32, "p (q c) -> p q c", q=8)
        ob = cut(8 * E * 4, F32, "p (q c) -> p q c", q=8)
        empty = sb("empty", [P, ROW], F16)

        const_made = sem("const_made")
        pool_step = sem("pool_step")
        w_in, sl_in, cst_in = sem("w_in"), sem("sl_in"), sem("cst_in")
        dve_step = sem("dve_step")
        act_step = sem("act_step")
        w_split = sem("w_split")
        x_in, x_made = sems("x_in"), sem("x_made")
        stats = sem("stats")
        std_made = sem("std_made")
        xw_made = sem("xw_made")
        t_made, t_used = sem("t_made"), sem("t_used")
        qk_made, hi_made, r1_made, mid_made, lo_made = (sem(n) for n in ("qk_made", "hi_made", "r1_made", "mid_made", "lo_made"))
        parts_out = sems("parts_out", 4)
        v_made, v_used = sem("v_made"), sem("v_used")
        v_out = sems("v_out")
        we_in, we_hi, we_lo, we_out = sems("we_in"), sem("we_hi"), sem("we_lo"), sems("we_out")
        q8 = sem("q8")
        rows_made, rows_in = sem("rows_made"), sem("rows_in")
        exp8 = sem("exp8")
        grp_in = [sems(f"grp_in{p}_", NG) for p in range(2)]
        vb_in = sems("vb_in")
        xr_in, xr_made, xa_out = sems("xr_in"), sem("xr_made"), sems("xa_out")
        sm_made, max_made = sem("sm_made"), sem("max_made")
        ct_made, c_made, c_in = sem("ct_made"), sem("c_made"), sems("c_in")
        s_made, exp_made, sel_made = sem("s_made"), sem("exp_made"), sem("sel_made")
        y_made, y_copied, y_normal = sem("y_made"), sem("y_copied"), sem("y_normal")
        pj_made, xadd_made = sem("pj_made"), sem("xadd_made")
        cnt_made, tot_made = sem("cnt_made"), sem("tot_made")
        rt_dve, rt_pe = sem("rt_dve"), sem("rt_pe")
        pos_made, scattered, list_init, w1_in, w2_in = sem("pos_made"), sem("scattered"), sem("list_init"), sem("w1_in"), sem("w2_in")
        xs_in, tt_made, xT_made, h_made, hg_made, hh_made, hl_made, o_made, ob_made = (
            sems("xs_in", SLOTS), sem("tt_made"), sem("xT_made"), sem("h_made"), sem("hg_made"), sem("hh_made"),
            sem("hl_made"), sem("o_made"), sem("ob_made"))
        xg_in, ob_out = sems("xg_in", SLOTS), sems("ob_out", SLOTS)
        empt = sem("empt")

        rec_step, rec_made = sem("rec_step"), sem("rec_made")
        shift_step = sem("shift_step")
        consts = sem("consts")
        apart = sem("apart")

        block = ctx.enter_context(nc.Block())

        def after(eng, signal, value):
            if not isinstance(value, int) or value > 0:
                eng.wait_ge(signal, value)

        def wait_apart(eng, signal, value):
            eng.wait_ge(signal, value)
            eng.sem_inc(apart, 1)

        def pairs(eng, count, body, first=0):
            with eng.Fori(first, first + count) as i:
                for p in range(2):
                    body(i * 2 + p, i, p)

        def rows_of_b(eng, body):
            body(0, 0, 0)
            with eng.Fori(0, (ROUTED - 1) // 2) as k:
                body(k * 2 + 1, k, 1)
                body(k * 2 + 2, k + 1, 0)
            for n in range(ROUTED, B):
                body(n, n // 2, n % 2)

        looped = lambda n: not isinstance(n, int)

        def is_row(n, row):
            return isinstance(n, int) and n == row

        def quarters_before(n, g, j):
            return n * (2 * NG) + (2 * g + j - 2 * NG)

        def expert_of(n, g):
            return n * 2 + (g // 2 - 2)

        def stage_a(eng, body, after_first=lambda: None):
            body(0, 0, 0, True)
            after_first()
            body(1, 0, 1, True)
            pairs(eng, B // 2 - 2, lambda n, i, p: body(n, i, p, True), 1)
            for n in (B - 2, B - 1):
                body(n, n // 2, n % 2, n < B - 1)

        def load_group(eng, n, p, g, which=(0, 1)):
            for w in which:
                st, part_d, runs = ((qs, qk_d[1], Q_RUNS), (ks, qk_d[0], K_RUNS))[w]
                for block, count, part, step in runs:
                    v = part_d[bass.ds(n, 1), part:part + (count if step else 1), :, g * HG * S:(g + 1) * HG * S] \
                        .rearrange("x s d c -> (x s) d c")
                    eng.dma_start(st[block * D:(block + count) * D, p, g].rearrange("p h n -> p (h n)"),
                                  v if step else v.broadcast_to([count, D, HG * S])).then_inc(grp_in[p][g], 16)

        @block.sync
        def _(sp):
            sp.dma_start(xin[0], x_t[0]).then_inc(x_in[0], 16)
            sp.dma_start(wk_f[:, :, 0:3 * E], w_kqv.rearrange("(k p) c -> p k c", p=P)).then_inc(w_in, 16)
            sp.dma_start(wk_f[:, :, 3 * E:], wg.rearrange("(k p) c -> p k c", p=P)).then_inc(w_in, 16)
            sp.dma_start(bqk[:, :], b_kqv[0:2 * E].rearrange("(c p) -> p c", p=P), allow_slow_non_contiguous=True).then_inc(w_in, 16)
            sp.dma_start(xin[1], x_t[1]).then_inc(x_in[1], 16)
            sp.dma_start(sl[R_ALIBI:R_ALIBI + 3, 0, :], slopes.partition_broadcast(3)).then_inc(sl_in, 16)
            sp.dma_start(bv[:, :, :].rearrange("p h d -> p (h d)"),
                         b_kqv[2 * E:3 * E].partition_broadcast(P)).then_inc(cst_in, 16)
            sp.dma_start(bp[:, :], b_proj.partition_broadcast(P)).then_inc(cst_in, 16)
            sp.wait_ge(const_made, 11)
            for j in range(HG):
                sp.dma_start(wp[32 * j:32 * j + D, :, :],
                             w_proj.rearrange("(g j d) n -> j d g n", g=NG, d=D)[j]).then_inc(cst_in, 16)

            def load_row(n, p):
                sp.dma_start(xin[p], x_t[bass.ds(n, 1)].rearrange("b p t e -> p (b t) e")).then_inc(x_in[p], 16)

            def a(n, i, p, more):
                if not isinstance(n, int) or n < B - 2:
                    sp.wait_ge(x_made, n + 1)
                    load_row(n + 2, p)
                for c in range(4):
                    sp.wait_ge(lo_made, 4 * n + c + 1)
                    h0 = (c % 2) * (H // 2)
                    for s in range(PARTS):
                        sp.dma_start(qk_d[c // 2][bass.ds(n, 1), s, :, h0 * S:(h0 + H // 2) * S]
                                     .rearrange("x d (h n) -> (x h) d n", n=S), pt[c][:, s, :]).then_inc(parts_out[c], 16)
                if not more or is_row(n, B - 2):
                    for c in range(4):
                        sp.wait_ge(parts_out[c], 16 * PARTS * n)
                    for g in ((2, 3) if not more else (0, 1)):
                        load_group(sp, 0, 0, g)
                sp.wait_ge(v_used, 4 * n + 4)
                sp.dma_start(v_d[bass.ds(n, 1)].rearrange("b p c -> p (b c)"),
                             vt[:, p].rearrange("p t h w -> p (t h w)")).then_inc(v_out[p], 16)

            stage_a(sp, a)

            def load_v(n, p):
                sp.dma_start(vt[:, p].rearrange("p t h w -> p (t h w)"),
                             v_d[bass.ds(n, 1)].rearrange("b p c -> p (b c)")).then_inc(vb_in[p], 16)

            def load_x(n, p):
                sp.dma_start(xr[:, p], x_t[bass.ds(n, 1)].rearrange("b p t e -> p (b t) e")).then_inc(xr_in[p], 16)

            for c in range(4):
                sp.wait_ge(parts_out[c], 16 * PARTS * B)
            for p in range(2):
                sp.wait_ge(v_out[p], 16 * B // 2)
            load_v(0, 0)
            sp.wait_ge(rows_made, NG)
            for st in (qs, ks):
                sp.dma_start(st[R_ALIBI:P, 1], st[R_ALIBI:P, 0]).then_inc(rows_in, 16)
            for g in range(NG):
                load_group(sp, 1, 1, g)
            load_x(0, 0)
            load_v(1, 1)
            load_x(1, 1)

            def load_quarter(n, g, j):
                expert = bass.ds(expert_of(n, g), 1)
                if g % 2 == 0:
                    sp.dma_start(wq[j], w1[expert, j * P:(j + 1) * P, :].rearrange("x p f -> p (x f)")).then_inc(we_in[j], 16)
                else:
                    sp.dma_start(wq[j].rearrange("p (k f) -> p k f", k=2),
                                 w2[expert, 2 * j * P:2 * (j + 1) * P, :]
                                 .rearrange("x (k p) f -> p (x k) f", p=P)).then_inc(we_in[j], 16)

            def store_quarter(n, g, j):
                expert = bass.ds(expert_of(n, g), 1)
                sp.wait_ge(we_lo, quarters_before(n, g, j) + 1)
                for part in range(2):
                    sp.dma_start(ws_d[expert, :, part, g % 2, j * 512:(j + 1) * 512].rearrange("x p w -> p (x w)"),
                                 wq_part[j][part]).then_inc(we_out[j], 16)

            def store_sum(n, p):
                sp.wait_ge(xadd_made, 2 * n + 2 + 1)
                sp.dma_start(xa_t[bass.ds(n, 1)].rearrange("b p t e -> p (b t) e"), xr[:, p]).then_inc(xa_out[p], 16)

            def b(n, i, p):
                first, last = is_row(n, 0), is_row(n, B - 1)
                for g in range(NG):
                    if looped(n):
                        for j in range(2):
                            load_quarter(n, g, j)
                        store_quarter(n, g, 0)
                    if g == 3 and not first:
                        store_sum(n - 1, 1 - p)
                        if not last:
                            sp.wait_ge(xa_out[1 - p], (i if p else i - 1) * 16 + 16)
                            load_x(n + 1, 1 - p)
                    if looped(n) or n < B - 2:
                        sp.wait_ge(s_made, NSJ * (NG * n + g + 1))
                        load_group(sp, n + 2, p, g)
                    if looped(n):
                        store_quarter(n, g, 1)
                    if g == 0 and not first and not last:
                        sp.wait_ge(y_made, NG * n + 2)
                        load_v(n + 1, 1 - p)
                    if g == 0 and last:
                        for j in range(2):
                            sp.wait_ge(we_out[j], 32 * X * 2 + 32)
                        sp.wait_ge(c_in[1], 32 * B // 2)
                        sp.wait_ge(s_made, NSJ * NG * (B - 1))
                        sp.dma_start(w2_h, ws_d[:, :, 0, 1, :].rearrange("x p w -> p x w")).then_inc(w2_in, 16)
                        sp.dma_start(w2_l, ws_d[:, :, 1, 1, :].rearrange("x p w -> p x w")).then_inc(w2_in, 16)
                        sp.wait_ge(scattered, 16 * NT)
                        for a_ in range(2):
                            sp.dma_start(w1_sb[:, :, a_, :], ws_d[:, :, a_, 0, :].rearrange("x p w -> p x w")).then_inc(w1_in, 16)

            rows_of_b(sp, b)

            def load_tile(s, k, q):
                sp.dma_start(xs_sb[:, q, :].bitcast(I32), xs_d[bass.ds(s * P, P), :]).then_inc(xs_in[q], 16)

            sp.wait_ge(y_made, NG * B + 2)
            for q in range(SLOTS):
                load_tile(q, 0, q)
            store_sum(B - 1, 1)
            with sp.Fori(1, TILES // SLOTS) as k:
                for q in range(SLOTS):
                    sp.wait_ge(ob_out[q], k * 16)
                    load_tile(k * SLOTS + q, k, q)
            for q in range(SLOTS):
                sp.wait_ge(ob_out[q], 16 * (TILES // SLOTS))

        @block.gpsimd
        def _(pool):
            step = [0]

            def mark(ins):
                step[0] += 1
                ins.then_inc(pool_step, 1)
                pool.wait_ge(pool_step, step[0])

            for m in (id16, idb, idf):
                pool.memset(m[:, :], 0.0).then_inc(pool_step, 1)
            step[0] += 3
            mark(pool.memset(epst[:, :], EPS))
            pool.sem_inc(const_made, 1)
            for m in (id16, idb, idf):
                pool.affine_select(out=m[:, :], in_=m[:, :], compare_op=ALU.not_equal, fill=1.0, base=0,
                                   pattern=[[-1, P]], channel_multiplier=1).then_inc(const_made, 1)
            pool.memset(ones[:, :], 1.0).then_inc(pool_step, 1)
            pool.memset(tri[:, :], 1.0).then_inc(pool_step, 1)
            pool.memset(maxmask[:, :], 0.0).then_inc(pool_step, 1)
            step[0] += 3
            mark(pool.memset(wp[:, :, :], 0.0))
            pool.affine_select(out=tri[:, :], in_=tri[:, :], compare_op=ALU.is_ge, fill=0.0, base=-1,
                               pattern=[[1, P]], channel_multiplier=-1).then_inc(const_made, 1)
            pool.affine_select(out=maxmask[:, :], in_=maxmask[:, :], compare_op=ALU.is_ge, fill=NEG, base=0,
                               pattern=[[-1, P]], channel_multiplier=1).then_inc(const_made, 1)
            pool.memset(seg[:, :, :], 1.0).then_inc(const_made, 1)
            for p in range(2):
                pool.memset(vt[:, p].rearrange("p t h w -> p (t h) w")[:, :, D:VW], 1.0).then_inc(const_made, 1)
            pool.memset(empty[:, :], 0.0).then_inc(const_made, 1)
            pool.memset(thr[:, :], 0.0).then_inc(const_made, 1)
            base = 11
            def ints(pattern, n, b0, out_ap, chan=0):
                mark(pool.iota(iot[:, 0:n], pattern=pattern, base=b0, channel_multiplier=chan))
                mark(pool.tensor_copy(out_ap, iot[:, 0:n]))

            ints([[-1, X], [0, NT]], X * NT, X, rank8[:, :, :].rearrange("p a b -> p (a b)"))
            ints([[0, X], [P, NT]], X * NT, 0, lim[:, :, :].rearrange("p a b -> p (a b)"))
            ints([[1, TILES], [0, X]], TILES * X, 0, sno[:, :, :].rearrange("p a b -> p (a b)"))
            mark(pool.iota(tok[:, :], pattern=[[P, NT]], base=0, channel_multiplier=1))
            pool.wait_ge(const_made, base)
            mark(pool.memset(seg[:, :, 0:1], 0.0))
            for k in range(BITS):
                pool.memset(bits[:, k, :], 1 << (BITS - 1 - k)).then_inc(pool_step, 1)
            step[0] += BITS
            for k in range(SLOTS):
                pool.memset(place[:, k:k + 1], float(X ** k)).then_inc(pool_step, 1)
            step[0] += SLOTS
            mark(pool.memset(empty[:, 2 * E:2 * E + 2].bitcast(I32), NO_TOKEN))
            pool.sem_inc(consts, 1)

            rows = slice(R_ALIBI, P)
            b0 = (R_FAR - 1 - R_ALIBI) * FAR
            mark(pool.memset(k_rows[rows, :], 1.0))
            mark(pool.affine_select(out=k_rows[rows, :], in_=k_rows[rows, :], compare_op=ALU.is_ge, fill=0.0, base=b0,
                                    pattern=[[1, S]], channel_multiplier=-FAR))
            mark(pool.affine_select(out=k_rows[rows, :], in_=k_rows[rows, :], compare_op=ALU.is_ge, fill=0.0,
                                    base=FAR - 1 - b0, pattern=[[-1, S]], channel_multiplier=FAR))
            mark(pool.memset(k_rows[R_ALIBI:R_FAR, :], 1.0))
            mark(pool.iota(posi[R_ALIBI:R_SHIFT, :], pattern=[[1, S]], base=-MID, channel_multiplier=0))
            mark(pool.tensor_copy(k_rows[R_ALIBI:R_SHIFT, :], posi[R_ALIBI:R_SHIFT, :]))
            mark(pool.memset(q_rows[rows, :], 0.0))
            mark(pool.affine_select(out=q_rows[rows, :], in_=q_rows[rows, :], compare_op=ALU.is_ge, fill=NEG, base=b0,
                                    pattern=[[1, S]], channel_multiplier=-FAR))
            pool.sem_inc(consts, 1)

            def a(n, i, p, more):
                for c in range(4):
                    pool.wait_ge(mid_made, 4 * n + c + 1)
                    pool.tensor_tensor(pt[c][:, 2, :], r1[c % 2], pt[c][:, 1, :], ALU.subtract).then_inc(lo_made, 1)

            stage_a(pool, a)

            def normalise(n, g):
                pool.wait_ge(rec_made, NG * n + g + 1)
                if g == 0:
                    pool.wait_ge(pj_made, 2 * n + 2)
                pool.tensor_tensor(yn[:, g, :], ysb[:, g % 2, :], rec_wide[:, g % 2, :], ALU.mult).then_inc(y_normal, 1)

            def scatter(t):
                pool.indirect_dma_start(out=xs_d, out_offset=bass.IndirectOffsetOnAxis(ap=pos[:, t:t + 1].bitcast(U32), axis=0),
                                        in_=xnp[:, t, :].bitcast(I32), in_offset=None).then_inc(scattered, 16)

            def b(n, i, p):
                first = is_row(n, 0)
                if is_row(n, ROUTED + 1):
                    pool.wait_ge(pos_made, 1)
                    pool.wait_ge(list_init, 16)
                for g in range(NG):
                    for h in range(HG):
                        wait_apart(pool, exp_made, NSJ * (NG * n + g) + 3 * (h + 1) + 3)
                        v = pr_all[:, HG * (g % 2) + h, 0:W_R0].rearrange("p (t q) -> p t q", t=TB)
                        pool.affine_select(out=v, in_=v, compare_op=ALU.is_ge, fill=0.0, base=0,
                                           pattern=[[0, TB], [1, P]], channel_multiplier=-1).then_inc(sel_made, 1)
                        if is_row(n, ROUTED + 1):
                            for j in range(2):
                                scatter(2 * (HG * g + h) + j)
                        if h == (3 if g == 2 else 1):
                            if g >= 2:
                                normalise(n, g - 2)
                            elif not first:
                                normalise(n - 1, g + 2)
                        if g == 1 and h == 3:
                            pool.wait_ge(xr_in[p], i * 16 + 16)
                            pool.tensor_tensor(xr[:, p], xr[:, p], bp[:, None, :].broadcast_to([P, TB, E]), ALU.add).then_inc(xr_made, 1)
                        if looped(n) and h >= 2:
                            j = h - 2
                            pool.wait_ge(we_hi, quarters_before(n, g, j) + 1)
                            pool.tensor_tensor(wq_part[j][1], wq[j], wq_part[j][0], ALU.subtract).then_inc(we_lo, 1)

            pool.wait_ge(exp_made, 3 + 1)
            pool.dma_start(xs_d.rearrange("(s p) c -> p s c", p=P),
                           empty[:, :].bitcast(I32)[:, None, :].broadcast_to([P, TILES, ROW // 2])).then_inc(list_init, 16)
            rows_of_b(pool, b)
            normalise(B - 1, 2)
            normalise(B - 1, 3)

            def tile_c(s, k, q):
                token = xs_sb[:, q, 2 * E:2 * E + 2].bitcast(U32)
                wait_apart(pool, xs_in[q], 16 * (k + 1))
                pool.indirect_dma_start(out=xg[:, q, :], out_offset=None, in_=xa_d,
                                        in_offset=bass.IndirectOffsetOnAxis(ap=token, axis=0),
                                        bounds_check=T - 1, oob_is_err=False).then_inc(xg_in[q], 16)

            def scatter_c(s, k, q):
                token = xs_sb[:, q, 2 * E:2 * E + 2].bitcast(U32)
                wait_apart(pool, ob_made, s + 1)
                pool.indirect_dma_start(out=out_rows, out_offset=bass.IndirectOffsetOnAxis(ap=token, axis=0),
                                        in_=ob[:, q, :], in_offset=None,
                                        bounds_check=T - 1, oob_is_err=False).then_inc(ob_out[q], 16)

            for p in range(2):
                pool.wait_ge(xa_out[p], 16 * B // 2)
            mark(pool.memset(xg[:, :, :], 0.0))
            for q in range(AHEAD):
                tile_c(q, 0, q)
            with pool.Fori(0, TILES // SLOTS - 1) as k:
                for q in range(SLOTS):
                    s2 = q + AHEAD
                    tile_c(k * SLOTS + s2, k + s2 // SLOTS, s2 % SLOTS)
                    scatter_c(k * SLOTS + q, k, q)
            k = TILES // SLOTS - 1
            for q in range(SLOTS):
                s2 = q + AHEAD
                if s2 < SLOTS:
                    tile_c(k * SLOTS + s2, k, s2)
                scatter_c(k * SLOTS + q, k, q)

        @block.scalar
        def _(act):
            act.sem_inc(exp_made, 3)
            for j in range(2):
                act.sem_inc(we_out[j], 32)
            act.sem_inc(y_copied, 1)
            def root(n):
                act.wait_ge(stats, n + 1)
                act.activation(std[:, :], mv[:, :, 1], ACT.Sqrt, bias=epst[:, 0:1]).then_inc(std_made, 1)

            act.wait_ge(const_made, 1)
            root(0)
            act.wait_ge(w_in, 48)
            act.activation(w_h[:, :, :], wk_f, ACT.Copy, scale=WS).then_inc(w_split, 1)
            act.activation(bqk[:, :], bqk[:, :], ACT.Copy, scale=WS).then_inc(act_step, 1)
            act.wait_ge(act_step, 1)
            def take_rows(n, p):
                act.wait_ge(t_made, n + 1)
                after(act, v_made, 4 * n - 4)
                for a_ in range(2):
                    act.activation(xt[p][:, a_].rearrange("p k n -> p (k n)"), bank[a_].bitcast(F16),
                                   ACT.Copy).then_inc(t_used, 1)

            def a(n, i, p, more):
                def hi(c):
                    act.wait_ge(qk_made, 4 * n + c + 1)
                    after(act, parts_out[c], 16 * PARTS * n)
                    act.activation(pt[c][:, 0, :], bank[2 + c], ACT.Identity, bias=bqk[:, c:c + 1]).then_inc(hi_made, 1)

                def mid(c):
                    act.wait_ge(r1_made, 4 * n + c + 1)
                    act.activation(pt[c][:, 1, :], r1[c % 2], ACT.Copy).then_inc(mid_made, 1)

                hi(0)
                for c in range(4):
                    if c < 3:
                        hi(c + 1)
                    mid(c)
                    if more and c == 2:
                        take_rows(n + 1, 1 - p)
                if looped(n) or n < B - 2:
                    root(n + 2)
                if p == 1:
                    if is_row(n, 1):
                        act.wait_ge(rows_in, 32)
                    act.activation(qs[R_ALIBI:R_SHIFT, 0, bass.ds(i, 1)].rearrange("p g h n -> p (g h) n"),
                                   sl[R_ALIBI:R_SHIFT, 6, bass.ds(i * HG, HG)][:, :, None].broadcast_to([3, HG, S]),
                                   ACT.Copy).then_inc(rows_made, 1)

            def constant_rows():
                act.wait_ge(q8, 1)
                act.wait_ge(consts, 2)
                for st, one in ((ks, k_rows), (qs, q_rows)):
                    act.dma_start(st[R_ALIBI:P, 0].rearrange("p g h n -> p (g h) n"),
                                  one[R_ALIBI:P, None, :].broadcast_to([P - R_ALIBI, H, S])).then_inc(rows_in, 16)

            take_rows(0, 0)
            act.wait_ge(w_split, 2)
            root(1)
            stage_a(act, a, constant_rows)

            act.wait_ge(q8, 2)
            act.activation(pe8[:, :, :], lg[:, :, :], ACT.Exp).then_inc(exp8, 1)

            def shift_rows(n1, p1):
                act.wait_ge(c_made, n1 + 1)
                for r in range(2):
                    act.dma_start(qs[R_SHIFT + r:R_SHIFT + r + 1, p1].rearrange("p g h n -> p (g h) n"),
                                  cc[:, r, :]).then_inc(c_in[p1], 16)

            def copy_y(n, g):
                act.wait_ge(y_made, NG * n + g + 1 + 2)
                act.wait_ge(y_normal, NG * n + g + 1)
                act.activation(ysb[:, g % 2, :], bank[5], ACT.Copy).then_inc(y_copied, 1)

            def b(n, i, p):
                for g in range(NG):
                    act.wait_ge(y_made, NG * n + g + 1)
                    for h in range(HG):
                        if not is_row(n, B - 1) and g == NG - 1 and h == 3:
                            shift_rows(n + 1, 1 - p)
                        buf = pr_all[:, HG * (g % 2) + h, :]
                        for j, (c0, w) in enumerate(((W_R0, 384), (W_R1, 384), (W_DIAG, 512))):
                            act.wait_ge(s_made, NSJ * (NG * n + g) + 3 * h + j + 1)
                            act.activation(buf[:, c0:c0 + w], bank[2 + j][:, 0:w], ACT.Exp, scale=SCORE)\
                               .then_inc(exp_made, 1)
                            if h == 3 and j == 1:
                                if g >= 1:
                                    copy_y(n, g - 1)
                                elif not is_row(n, 0):
                                    copy_y(n - 1, NG - 1)
                        if looped(n) and h >= 2:
                            j = h - 2
                            act.wait_ge(we_in[j], n * (16 * NG) + 16 * (g - NG) + 16)
                            act.wait_ge(we_out[j], n * (32 * NG) + 32 * (g - NG) + 32)
                            act.activation(wq_part[j][0], wq[j], ACT.Copy, scale=WS)
                            act.activation(wq[j], wq[j], ACT.Copy, scale=WS).then_inc(we_hi, 1)

            act.wait_ge(rows_in, 64)
            shift_rows(0, 0)
            rows_of_b(act, b)
            copy_y(B - 1, NG - 1)

            def gelu(s, q):
                act.wait_ge(h_made, s + 1)
                after(act, hl_made, s - 1)
                act.activation(hg[:, q, :], bank[2 + q], ACT.Gelu, scale=1.0 / WS).then_inc(hg_made, 1)
                act.wait_ge(hg_made, s + 1)
                after(act, o_made, s - 1)
                act.activation(hh[:, q, 0, :], hg[:, q, :], ACT.Copy).then_inc(hh_made, 1)

            gelu(0, 0)
            gelu(1, 1)
            with act.Fori(1, TILES // 2) as k:
                for q in range(2):
                    gelu(2 * k + q, q)

        @block.vector
        def _(dve):
            step = [0]

            def mark(ins):
                step[0] += 1
                ins.then_inc(dve_step, 1)
                dve.wait_ge(dve_step, step[0])

            dve.sem_inc(y_normal, 2)
            dve.sem_inc(xadd_made, 1)
            A_STEPS = 4
            before = [0]

            def link(ins, n, k):
                ins.then_inc(dve_step, 1)
                wait_apart(dve, dve_step, n * A_STEPS + (before[0] + k))

            def measure(n, i, p):
                dve.wait_ge(x_in[p], i * 16 + 16)
                for t in range(TB):
                    last = dve.bn_stats(bst[:, t, :], xin[p][:, t, :])
                link(last, n, 1)
                for t in range(TB):
                    last = dve.bn_aggr(mv[:, t, :], bst[:, t, :])
                last.then_inc(stats, 1)

            def normal_rows(n, i, p):
                dve.wait_ge(std_made, n + 1)
                link(dve.reciprocal(rstd[:, :], std[:, :]), n, 2)
                after(dve, xw_made, n)
                for t in range(TB):
                    last = dve.tensor_scalar(xn[:, t, :], xin[p][:, t, :], mv[:, t, 0:1], rstd[:, t:t + 1],
                                             ALU.subtract, ALU.mult)
                link(last, n, 3)
                dve.sem_inc(x_made, 1)
                v = xnp[:, bass.ds(n * TB, TB), :]
                link(dve.tensor_copy(v[:, :, 0:E], xn), n, 4)
                dve.tensor_tensor(v[:, :, E:2 * E], xn, v[:, :, 0:E], ALU.subtract).then_inc(xw_made, 1)

            def a(n, i, p, more):
                def rest(c):
                    dve.wait_ge(hi_made, 4 * n + c + 1)
                    after(dve, lo_made, 4 * n + c - 1)
                    dve.scalar_tensor_tensor(out=r1[c % 2], in0=bank[2 + c], scalar=bqk[:, c:c + 1],
                                             in1=pt[c][:, 0, :], op0=ALU.add, op1=ALU.subtract).then_inc(r1_made, 1)

                if more:
                    normal_rows(n + 1, i + p, 1 - p)
                rest(0)
                rest(1)
                rest(2)
                rest(3)
                if looped(n) or n < B - 2:
                    measure(n + 2, i + 1, p)
                after(dve, v_out[p], 16 * i)
                for t in range(TB):
                    dve.wait_ge(v_made, 4 * n + t + 1)
                    vb = bank[6 + t % 2]
                    dve.scalar_tensor_tensor(out=vt[:, p, t, :, 0:D], in0=vb[:, 0:E].rearrange("p (h d) -> p h d", h=H),
                                             scalar=1.0 / WS, in1=bv[:, :, :], op0=ALU.mult, op1=ALU.add)
                    dve.tensor_scalar(lg[:, bass.ds(4 * n + t, 1), :].rearrange("p a b -> p (a b)"), vb[:, E:E + X],
                                      1.0 / WS, None, ALU.mult).then_inc(v_used, 1)

            measure(0, 0, 0)
            normal_rows(0, 0, 0)
            step[0] = A_STEPS
            dve.wait_ge(w_split, 1)
            mark(dve.scalar_tensor_tensor(out=w_l[:, :, :], in0=wk_f, scalar=WS, in1=w_h[:, :, :],
                                          op0=ALU.mult, op1=ALU.subtract))
            dve.sem_inc(w_split, 1)
            dve.wait_ge(sl_in, 16)
            mark(dve.tensor_scalar(sl[R_ALIBI:R_SHIFT, 1, :], sl[R_ALIBI:R_SHIFT, 0, :], 1.0 / SCORE, None, ALU.mult))
            al = slice(R_ALIBI, R_SHIFT)
            dve.wait_ge(const_made, 4)
            for r in range(3):
                mark(dve.tensor_copy(slb[al, r, :], sl[al, 1 + r, :]))
                if r < 2:
                    mark(dve.tensor_tensor(sl[al, 2 + r, :], sl[al, 1 + r, :], slb[al, r, :], ALU.subtract))
            mark(dve.tensor_scalar(sl[al, 4, :], slb[al, 0, :], idf[al, R_ALIBI:R_ALIBI + 1], None, ALU.mult))
            for r in (1, 2):
                mark(dve.scalar_tensor_tensor(out=sl[al, 4 + r, :], in0=slb[al, r, :],
                                              scalar=idf[al, R_ALIBI + r:R_ALIBI + r + 1],
                                              in1=sl[al, 3 + r, :], op0=ALU.mult, op1=ALU.add))
            dve.sem_inc(q8, 1)
            before[0] = step[0] - A_STEPS
            measure(1, 0, 1)
            dve.wait_ge(cst_in, 96)
            stage_a(dve, a)
            step[0] += A_STEPS * (B - 1)

            dve.wait_ge(v_used, NT)
            dve.wait_ge(consts, 1)
            bc = lambda ap: ap[:, :, None].broadcast_to([P, NT, X])
            mark(dve.tensor_reduce(r32[:, 0, :], lg[:, :, :], AX, ALU.max))
            mark(dve.tensor_tensor(lg[:, :, :], lg[:, :, :], bc(r32[:, 0, :]), ALU.subtract))
            dve.sem_inc(q8, 1)
            dve.memset(bank[5], 0.0).then_inc(y_copied, 1)
            dve.wait_ge(exp8, 1)
            mark(dve.tensor_reduce(r32[:, 1, :], pe8[:, :, :], AX, ALU.add))
            mark(dve.reciprocal(r32[:, 2, :], r32[:, 1, :]))
            mark(dve.tensor_tensor(pr[:, :, :].rearrange("p e t -> p t e"), pe8[:, :, :], bc(r32[:, 2, :]), ALU.mult))

            def row_max(n1, p1, g, k):
                u = NU * (NG * n1 + g) + k
                qt, hs = UNITS[k]
                w = (qt + 1) * P
                dve.wait_ge(sm_made, u + 1)
                src = bank[(NU * g + k) % 2][:, 0:w * len(hs)].rearrange("p (h c) -> p h c", c=w)
                h0 = g * HG + hs[0]
                dve.tensor_reduce(mx[:, p1, qt, h0:h0 + len(hs)], src, AX, ALU.max).then_inc(max_made, 1)

            def make_shift(n1, p1):
                dve.wait_ge(ct_made, n1 + 1)
                dve.tensor_scalar(cc[:, 0, :], bank[7][0:H, :], -1.0, None, ALU.mult).then_inc(shift_step, 1)
                dve.wait_ge(shift_step, n1 + 1)
                dve.scalar_tensor_tensor(out=cc[:, 1, :], in0=bank[7][0:H, :], scalar=-1.0, in1=cc[:, 0, :],
                                         op0=ALU.mult, op1=ALU.subtract).then_inc(c_made, 1)

            def invert(n, g):
                k0 = 2 * (NG * n + g)
                dve.wait_ge(y_copied, NG * n + g + 3)
                dve.transpose(yt[:, :, :].rearrange("p b c -> p (b c)"), ysb[:, g % 2, :]).then_inc(rec_step, 1)
                dve.wait_ge(rec_step, k0 + 1)
                dve.reciprocal(rec[:, :], yt[:, :, D]).then_inc(rec_step, 1)
                dve.wait_ge(rec_step, k0 + 2)
                dve.wait_ge(y_normal, NG * n + g + 1)
                dve.transpose(rec_wide[:, g % 2, :], rec[:, :, None].broadcast_to([P, S // 32, 32])
                              ).then_inc(rec_made, 1)

            def residual(n, p, j, src):
                if j == 0:
                    dve.wait_ge(xr_made, n + 1)
                dve.wait_ge(pj_made, 2 * n + j + 1 + 2)
                v = xr[:, p, 2 * j:2 * j + 2, :]
                dve.tensor_tensor(v, src.rearrange("p (t e) -> p t e", t=2), v, ALU.add).then_inc(xadd_made, 1)

            bisect_base = step[0]

            def bisect_count(it):
                k0 = bisect_base + 4 * it
                dve.tensor_tensor(cand[:, :].bitcast(U32), thr[:, :].bitcast(U32),
                                  bits[:, bass.ds(it, 1), :].rearrange("p a e -> p (a e)"),
                                  ALU.bitwise_or).then_inc(dve_step, 1)
                dve.wait_ge(dve_step, k0 + 1)
                dve.tensor_tensor(hit[:, :, :], pr[:, :, :], cand[:, :, None].broadcast_to([P, X, NT]),
                                  ALU.is_ge).then_inc(dve_step, 1)
                dve.wait_ge(dve_step, k0 + 2)
                with nc.allow_low_precision("counts up to 32 are exact"):
                    dve.tensor_reduce(cnt[:, :], hit[:, :, :], AX, ALU.add).then_inc(cnt_made, 1)

            def bisect_take(it):
                k0 = bisect_base + 4 * it
                dve.wait_ge(tot_made, it + 1)
                dve.tensor_scalar(acc[:, :], bank[7][:, 0:X], float(CAP), None, ALU.is_ge).then_inc(dve_step, 1)
                wait_apart(dve, dve_step, k0 + 3)
                dve.copy_predicated(thr[:, :], acc[:, :], cand[:, :]).then_inc(dve_step, 1)
                dve.wait_ge(dve_step, k0 + 4)

            for g in range(NG):
                for k in range(NU):
                    row_max(0, 0, g, k)
            make_shift(0, 0)

            e8 = lambda ap: ap[:, :, None].broadcast_to([P, X, NT])
            t32 = lambda ap: ap[:, None, :].broadcast_to([P, X, NT])
            by_t = lambda ap: ap[:, :, :].rearrange("p e t -> p t e")
            TT = lambda *a, **k: mark(dve.tensor_tensor(*a, **k))

            def offsets(dst, k):
                dve.wait_ge(rt_pe, k)
                mark(dve.tensor_copy(rr[2][:, :, :], bank[7][:, 256:512].rearrange("p (e t) -> p e t", e=X)))
                fl = lambda a_: a_[:, :, :].rearrange("p e t -> p (e t)")
                mark(dve.tensor_tensor_scan(fl(dst), fl(seg), fl(rr[2]), 0.0, ALU.mult, ALU.add))
                mark(dve.tensor_copy(r8[:, 2, :], dst[:, :, NT - 1]))
                TT(dst[:, :, :], dst[:, :, :], rr[2][:, :, :], ALU.subtract)
                TT(dst[:, :, :], bank[7][:, 0:256].rearrange("p (e t) -> p e t", e=X), dst[:, :, :], ALU.add)

            def mark_ties():
                TT(gtb[:, :, :], pr[:, :, :], e8(thr), ALU.is_gt)
                with nc.allow_low_precision("counts up to 32 are exact"):
                    mark(dve.tensor_reduce(cnt[:, :], gtb[:, :, :], AX, ALU.add))
                TT(hit[:, :, :], pr[:, :, :], e8(thr), ALU.is_equal)
                dve.sem_inc(rt_dve, 1)

            def pick():
                offsets(rr[0], 1)
                mark(dve.tensor_scalar(r8[:, 0, :], bank[6][:, 0:X], -1.0, float(CAP), ALU.mult, ALU.add))
                TT(rr[0][:, :, :], rr[0][:, :, :], e8(r8[:, 0, :]), ALU.is_lt)
                TT(rr[0][:, :, :], rr[0][:, :, :], hit[:, :, :], ALU.mult)
                TT(rr[0][:, :, :], rr[0][:, :, :], gtb[:, :, :], ALU.max)

            def rank():
                mark(dve.tensor_reduce(r32[:, 0, :], by_t(rr[0]), AX, ALU.max))
                TT(rr[0][:, :, :], rr[0][:, :, :], t32(r32[:, 0, :]), ALU.is_ge)
                TT(rr[1][:, :, :], rr[0][:, :, :], pr[:, :, :], ALU.mult)
                mark(dve.scalar_tensor_tensor(out=rr[1][:, :, :], in0=rr[0][:, :, :], scalar=-1.0, in1=rr[1][:, :, :],
                                              op0=ALU.add, op1=ALU.add))
                mark(dve.tensor_reduce(r32[:, 1, :], by_t(rr[1]), AX, ALU.max))
                TT(rr[1][:, :, :], rr[1][:, :, :], t32(r32[:, 1, :]), ALU.is_equal)

            def choose():
                TT(rr[1][:, :, :], rr[1][:, :, :], rank8[:, :, :], ALU.mult)
                mark(dve.tensor_reduce(r32[:, 2, :], by_t(rr[1]), AX, ALU.max))
                TT(hit[:, :, :], rr[1][:, :, :], t32(r32[:, 2, :]), ALU.is_equal)
                dve.sem_inc(rt_dve, 1)

            def weigh():
                TT(rr[1][:, :, :], hit[:, :, :], pr[:, :, :], ALU.mult)
                mark(dve.tensor_reduce(r32[:, 3, :], by_t(rr[1]), AX, ALU.max))
                mark(dve.tensor_scalar(r32[:, 3, :], r32[:, 3, :], 1.0 / WS, None, ALU.mult))
                offsets(rr[0], 2)

            def lay_tiles():
                TT(rr[1][:, :, :], e8(r8[:, 2, :]), lim[:, :, :], ALU.is_gt)
                mark(dve.tensor_reduce(r8[:, 3, :], rr[1][:, :, :], AX, ALU.add))
                mark(dve.memset(r8[:, 0, :], 1.0))
                mark(dve.tensor_tensor_scan(r8[:, 4, :], r8[:, 0, :], r8[:, 3, :], 0.0, ALU.mult, ALU.add))
                TT(r8[:, 5, :], r8[:, 4, :], r8[:, 3, :], ALU.subtract)
                mark(dve.tensor_scalar(r8[:, 5, :], r8[:, 5, :], float(P), None, ALU.mult))

            def place_tokens():
                TT(rr[0][:, :, :], rr[0][:, :, :], e8(r8[:, 5, :]), ALU.add)
                TT(rr[0][:, :, :], rr[0][:, :, :], hit[:, :, :], ALU.mult)
                mark(dve.tensor_reduce(r32[:, 4, :], by_t(rr[0]), AX, ALU.add))
                mark(dve.tensor_copy(pos[:, :], r32[:, 4, :]))
                mark(dve.tensor_copy(xnp[:, :, 2 * E:2 * E + 2].bitcast(I32).rearrange("p t a -> p (t a)"), tok[:, :]))
                mark(dve.tensor_copy(xnp[:, :, 2 * E + 2:].bitcast(F32).rearrange("p t a -> p (t a)"), r32[:, 3, :]))
                dve.sem_inc(pos_made, 1)

            def list_experts():
                TT(ecmp[:, :, :], r8[:, 4, :][:, None, :].broadcast_to([P, TILES, X]), sno[:, :, :], ALU.is_le)
                mark(dve.tensor_reduce(eidf[:, :], ecmp[:, :, :], AX, ALU.add))
                mark(dve.tensor_scalar(eidf[:, :], eidf[:, :], float(X - 1), None, ALU.min))
                groups = lambda ap: ap.rearrange("p (a s) -> p a s", s=SLOTS)
                TT(groups(eidf[:, :]), groups(eidf[:, :]), place[:, None, :].broadcast_to([P, TILES // SLOTS, SLOTS]),
                   ALU.mult)
                mark(dve.tensor_reduce(r8[:, 0, 0:TILES // SLOTS], groups(eidf[:, :]), AX, ALU.add))
                mark(dve.tensor_copy(codes[:, :], r8[:, 0, 0:TILES // SLOTS]))
                dve.sem_inc(pos_made, 1)

            routing = {(0, 1): mark_ties, (0, 9): pick, (1, 4): rank, (1, 9): choose, (2, 4): weigh,
                       (2, 9): lay_tiles, (3, 2): place_tokens, (3, 6): list_experts}

            def b(n, i, p):
                first, last, routed = is_row(n, 0), is_row(n, B - 1), is_row(n, ROUTED)
                bis = looped(n) or first
                if routed:
                    step[0] = bisect_base + 4 * BITS
                for g in range(NG):
                    it = n * BPB + sum(BIS[:g])
                    if bis:
                        bisect_count(it)
                    for k in range(NSJ):
                        u = NSJ * g + k
                        for m in UNITS_AT(u) if not last else ():
                            row_max(n + 1, 1 - p, m // NU, m % NU)
                        if not last and u == TURN:
                            make_shift(n + 1, 1 - p)
                        if k == 3 and g >= 2:
                            invert(n, g - 2)
                        if k == 3 and g < 2 and not first:
                            invert(n - 1, g + 2)
                        if g == 2 and k in (1, 8) and not first:
                            residual(n - 1, 1 - p, k // 8, bank[6])
                        if bis and k == COUNT_AT[g] + 1:
                            bisect_take(it)
                            if BIS[g] == 2:
                                bisect_count(it + 1)
                        if bis and k == 9 and BIS[g] == 2:
                            bisect_take(it + 1)
                        if routed and (g, k) in routing:
                            routing[g, k]()

            rows_of_b(dve, b)
            for g in (2, 3):
                invert(B - 1, g)
            for j in range(2):
                residual(B - 1, 1, j, bank[6 + j])

            def take_x(s, q):
                dve.wait_ge(tt_made, s + 1)
                dve.tensor_copy(xT[:, q].rearrange("p a n -> p (a n)"), bank[q].bitcast(F16)[:, 0:512]).then_inc(xT_made, 1)

            def low(s, q):
                dve.wait_ge(hh_made, s + 1)
                dve.tensor_tensor(hh[:, q, 1, :], hg[:, q, :], hh[:, q, 0, :], ALU.subtract).then_inc(hl_made, 1)

            def combine(s, k, q):
                dve.wait_ge(o_made, s + 1)
                dve.wait_ge(xg_in[q], k * 16 + 16)
                after(dve, ob_out[q], k * 16)
                dve.scalar_tensor_tensor(out=ob[:, q, :], in0=bank[4 + q % 2][:, 0:E],
                                         scalar=xs_sb[:, q, 2 * E + 2:].bitcast(F32), in1=xg[:, q, :],
                                         op0=ALU.mult, op1=ALU.add).then_inc(ob_made, 1)

            def steps(s, k, tiles, more=SLOTS):
                for q in range(tiles):
                    combine(s + q, k, q)
                    if q < more + 1:
                        low(s + q + 1, (q + 1) % 2)
                    if q < more - 1 or more == SLOTS:
                        take_x(s + q + 3, (q + 1) % 2)

            take_x(0, 0)
            take_x(1, 1)
            low(0, 0)
            take_x(2, 0)
            steps(0, 0, SLOTS)
            with dve.Fori(1, TILES // SLOTS - 1) as k:
                steps(k * SLOTS, k, SLOTS)
            steps(TILES - SLOTS, TILES // SLOTS - 1, SLOTS, SLOTS - 2)

        @block.tensor
        def _(pe):
            pe.sem_inc(y_made, 2)
            pe.sem_inc(pj_made, 2)
            pe.wait_ge(const_made, 4)
            pe.wait_ge(w_split, 2)

            def six(out, lhs, rhs):
                terms = [(0, 0), (0, 1), (1, 0)]
                for k in range(EC):
                    for j, (a_, b_) in enumerate(terms):
                        last = pe.matmul(out, lhs(a_, k), rhs(b_, k), start=(k == 0 and j == 0),
                                         stop=(k == EC - 1 and j == 2))
                return last

            def turn_rows(n, p):
                pe.wait_ge(xw_made, n + 1)
                after(pe, t_used, 2 * n)
                for t in range(TB):
                    for a_ in range(2):
                        for k in range(EC):
                            last = pe.transpose(bank[a_].bitcast(F16)[:, k * S + t * P:k * S + (t + 1) * P],
                                                xnp[:, bass.ds(n * TB + t, 1), (a_ * EC + k) * P:(a_ * EC + k + 1) * P]
                                                .rearrange("p t c -> p (t c)"), id16[:, :])
                last.then_inc(t_made, 1)

            def a(n, i, p, more):
                pe.wait_ge(t_used, 2 * n + 2)
                W = (w_h, w_l)
                for c in range(4):
                    after(pe, r1_made, 4 * n + c - 3)
                    six(bank[2 + c], lambda a_, k: W[a_][:, k, c * P:(c + 1) * P],
                        lambda b_, k: xt[p][:, b_, k, :]).then_inc(qk_made, 1)
                if more:
                    turn_rows(n + 1, 1 - p)
                for t in range(TB):
                    after(pe, v_used, 4 * n + t - 1)
                    last = six(bank[6 + t % 2][:, 0:E + X], lambda a_, k: xt[p][:, a_, k, t * P:(t + 1) * P],
                               lambda b_, k: W[b_][:, k, 2 * E:3 * E + X])
                    last.then_inc(v_made, 1)

            turn_rows(0, 0)
            stage_a(pe, a)
            pe.wait_ge(r1_made, 4 * B)
            pe.wait_ge(v_used, 4 * B)
            pe.wait_ge(y_copied, 2)

            def max_unit(n1, p1, i1, g, k):
                u = NU * (NG * n1 + g) + k
                if k == 0:
                    pe.wait_ge(grp_in[p1][g], i1 * (16 * RUNS) + 16 * RUNS)
                if not isinstance(n1, int) or u >= 2:
                    pe.wait_ge(max_made, u - 1)
                qt, hs = UNITS[k]
                w = (qt + 1) * P
                dst = bank[(NU * g + k) % 2]
                for j, h in enumerate(hs):
                    pe.matmul(dst[:, j * w:(j + 1) * w], qs[0:R_SHIFT, p1, g, h, qt * P:w],
                              ks[0:R_SHIFT, p1, g, h, 0:w], start=True, stop=False)
                    last = pe.matmul(dst[:, (j + 1) * w - P:(j + 1) * w], idb[:, :], maxmask[:, :],
                                     start=False, stop=True)
                last.then_inc(sm_made, 1)

            def scores(n, p, i, g, h, j):
                v = NSJ * (NG * n + g) + 3 * h + j
                if g == 0 and h == 0 and j == 0:
                    pe.wait_ge(c_in[p], 32 * (i + 1))
                pe.wait_ge(exp_made, v + 1)
                blocks = ([(0, P, 384, 0)], [(1, 2 * P, 256, 0), (2, 3 * P, P, 256)],
                          [(t, t * P, P, t * P) for t in range(TB)])[j]
                for t, q0, w, c0 in blocks:
                    last = pe.matmul(bank[2 + j][:, c0:c0 + w], ks[:, p, g, h, t * P:(t + 1) * P],
                                     qs[:, p, g, h, q0:q0 + w], start=True, stop=True)
                last.then_inc(s_made, 1)

            def with_v(n, p, i, g, k):
                if k == 0:
                    pe.wait_ge(sel_made, HG * (NG * n + g + 1))
                    pe.wait_ge(exp_made, NSJ * (NG * n + g + 1) + 3)
                    pe.wait_ge(y_copied, NG * n + g + 2)
                    if g == 0:
                        pe.wait_ge(vb_in[p], 16 * (i + 1))
                t, c0, q0, w = PIECES[k]
                for h in range(HG):
                    last = pe.matmul(bank[5][32 * h:32 * h + VW, q0:q0 + w], vt[:, p, t, g * HG + h, :],
                                     pr_all[:, HG * (g % 2) + h, c0:c0 + w], start=(k == 0),
                                     stop=(k == len(PIECES) - 1), skip_group_check=True)
                if k == len(PIECES) - 1:
                    last.then_inc(y_made, 1)

            def turn_max(n1, p1):
                pe.wait_ge(max_made, NU * NG * (n1 + 1))
                for t in range(TB):
                    last = pe.transpose(bank[7][0:H, t * P:(t + 1) * P], mx[:, p1, t, :], idf[:, :])
                last.then_inc(ct_made, 1)

            def project(n, j, ts, groups, dst):
                pe.wait_ge(y_normal, NG * n + groups[-1] + 1 + 2)
                for t in ts:
                    for g in groups:
                        last = pe.matmul(dst[:, t * E:(t + 1) * E], yn[:, g, (2 * j + t) * P:(2 * j + t + 1) * P],
                                         wp[:, g, :], start=(g == 0 and t == ts[0]), stop=(g == NG - 1),
                                         skip_group_check=True)
                if ts[-1] == 1 and groups[-1] == NG - 1:
                    last.then_inc(pj_made, 1)

            def total(it):
                pe.wait_ge(cnt_made, it + 1)
                pe.matmul(bank[7][:, 0:X], ones[:, :], cnt[:, :], start=True, stop=True).then_inc(tot_made, 1)

            pe.wait_ge(rows_made, NG)
            pe.wait_ge(const_made, 11)
            pe.wait_ge(cst_in, 96)
            for g in range(NG):
                for k in range(NU):
                    max_unit(0, 0, 0, g, k)
            turn_max(0, 0)
            pe.wait_ge(c_made, 1)
            pe.wait_ge(rows_in, 64)

            def count_marks(k):
                pe.wait_ge(rt_dve, k)
                v = hit[:, :, :].rearrange("p e t -> p (e t)")
                pe.matmul(bank[7][:, 0:256], tri[:, :], v, start=True, stop=True)
                last = pe.matmul(bank[7][:, 256:512], ones[:, :], v, start=True, stop=True)
                if k == 1:
                    last = pe.matmul(bank[6][:, 0:X], ones[:, :], cnt[:, :], start=True, stop=True)
                last.then_inc(rt_pe, 1)

            def b(n, i, p):
                first, last = is_row(n, 0), is_row(n, B - 1)
                bis = looped(n) or first
                for g in range(NG):
                    it = n * BPB + sum(BIS[:g])
                    for k in range(NSJ):
                        u = NSJ * g + k
                        for m in UNITS_AT(u) if not last else ():
                            max_unit(n + 1, 1 - p, i + p, m // NU, m % NU)
                        if not last and u == TURN:
                            turn_max(n + 1, 1 - p)
                        if u == 0 and not first:
                            pe.wait_ge(c_made, n + 1)
                        scores(n, p, i, g, k // 3, k % 3)
                        if bis and k == COUNT_AT[g]:
                            total(it)
                        if bis and k == 8 and BIS[g] == 2:
                            total(it + 1)
                        if is_row(n, ROUTED) and (g, k) in ((0, 4), (2, 0)):
                            count_marks(1 + g // 2)
                        if 4 <= k <= 10 and g >= 1:
                            with_v(n, p, i, g - 1, k - 4)
                        if 4 <= k <= 10 and g == 0 and not first:
                            with_v(n - 1, 1 - p, None, NG - 1, k - 4)
                        if (g, k) in PROJECT and not first:
                            j, t = PROJECT[g, k]
                            if t == 0:
                                pe.wait_ge(xadd_made, 2 * n + (j - 1))
                            project(n - 1, j, (t,), range(NG), bank[6])

            rows_of_b(pe, b)
            for k in range(len(PIECES)):
                with_v(B - 1, 1, None, NG - 1, k)
            pe.wait_ge(xadd_made, 2 * B - 1)
            for groups in ((0, 1, 2), (3,)):
                for j in range(2):
                    project(B - 1, j, (0, 1), groups, bank[6 + j])

            def turn_x(s, k, q):
                pe.wait_ge(xs_in[q], k * 16 + 16)
                for j in range(4):
                    last = pe.transpose(bank[q % 2].bitcast(F16)[:, j * P:(j + 1) * P], xs_sb[:, q, j * P:(j + 1) * P], id16[:, :])
                last.then_inc(tt_made, 1)

            def experts_of(k, count=SLOTS):
                code = pe.value_load(codes[0:1, bass.ds(k, 1)], min_val=0, max_val=X ** SLOTS - 1)
                return [pe.snap((code // X ** j) % X, min_val=0, max_val=X - 1) for j in range(count)]

            def up(s, q, e):
                pe.wait_ge(xT_made, s + 1)
                after(pe, hg_made, s - 1)
                terms = [(0, 0), (0, 1), (1, 0)]
                for f in range(FC):
                    for k in range(EC):
                        for j, (a_, b_) in enumerate(terms):
                            c0 = k * FF + f * P
                            last = pe.matmul(bank[2 + q][:, f * P:(f + 1) * P],
                                             w1_sb[:, bass.ds(e, 1), a_, c0:c0 + P].rearrange("p x w -> p (x w)"),
                                             xT[:, q, b_ * EC + k, :], start=(k == 0 and j == 0),
                                             stop=(k == EC - 1 and j == 2))
                last.then_inc(h_made, 1)

            def down(s, q, e):
                pe.wait_ge(hl_made, s + 1)
                after(pe, ob_made, s - 1)
                w2p = (w2_h, w2_l)
                for f in range(FC):
                    for j, (a_, b_) in enumerate([(0, 0), (0, 1), (1, 0)]):
                        last = pe.matmul(bank[4 + q][:, 0:E], hh[:, q, a_, f * P:(f + 1) * P],
                                         w2p[b_][:, bass.ds(e, 1), f * E:(f + 1) * E].rearrange("p x w -> p (x w)"),
                                         start=(f == 0 and j == 0), stop=(f == FC - 1 and j == 2))
                last.then_inc(o_made, 1)

            pe.wait_ge(w1_in, 32)
            pe.wait_ge(w2_in, 32)
            pe.wait_ge(pos_made, 2)
            def steps(s, k, more=SLOTS):
                experts = experts_of(k) + (experts_of(k + 1, 2) if more == SLOTS else [])
                for q in range(SLOTS):
                    down(s + q, q % 2, experts[q])
                    if q < more:
                        up(s + q + 2, q % 2, experts[q + 2])
                    if q < more - 1 or more == SLOTS:
                        turn_x(s + q + 3, k + (q + 3) // SLOTS, (q + 3) % SLOTS)

            first = experts_of(0, 2)
            turn_x(0, 0, 0)
            turn_x(1, 0, 1)
            up(0, 0, first[0])
            turn_x(2, 0, 2)
            up(1, 1, first[1])
            steps(0, 0)
            with pe.Fori(1, TILES // SLOTS - 1) as k:
                steps(k * SLOTS, k)
            steps(TILES - SLOTS, TILES // SLOTS - 1, SLOTS - 2)


_INS = ['L0_attn_x', 'L0_attn_W_kqv', 'L0_attn_b_kqv', 'L0_attn_W_proj', 'L0_attn_b_proj', 'L0_attn_slopes',
        'L0_ffn_Wg', 'L0_ffn_W1', 'L0_ffn_W2']


def kernel(**inputs):
    import numpy as _np
    import concourse.bacc as _bacc
    from concourse import mybir as _mybir
    from concourse.bass_utils import run_bass_kernel_spmd as _run

    nc = _bacc.Bacc("TRN2", target_bir_lowering=False, num_devices=1)
    arrays, args = {}, []
    for name in _INS:
        a = _np.ascontiguousarray(inputs[name])
        arrays[f"in_{name}_dram"] = a
        args.append(nc.dram_tensor(f"in_{name}_dram", a.shape, _mybir.dt.from_np(a.dtype), kind="ExternalInput").ap())
    args.append(nc.dram_tensor("out_0_dram", (B, S, E), _mybir.dt.float32, kind="ExternalOutput").ap())
    layer(nc, *args)
    r = _run(nc, [arrays], core_ids=[0])
    return r.results[0]["out_0_dram"]
```
